# Optimizing a Trainium2 kernel written in Bass

```python
import numpy as np
import jax
import jax.numpy as jnp

def _softmax(x, axis=-1):
    return jax.nn.softmax(x, axis=axis)
def _gelu(x):
    return jax.nn.gelu(x, approximate=True)
def _silu(x):
    return jax.nn.silu(x)
def _sigmoid(x):
    return jax.nn.sigmoid(x)
def _layernorm(x, axis=-1, eps=1e-5):
    m = jnp.mean(x, axis=axis, keepdims=True)
    v = jnp.var(x, axis=axis, keepdims=True)
    return (x - m) / jnp.sqrt(v + eps)
def _scatter_add(tgt, idx, src, axis=0):
    return tgt.at[idx].add(src)
def _segment_sum(src, seg, n):
    return jax.ops.segment_sum(src, seg, n)

kernel_name = 'mk_conv_preact_d2_conv_nhwc192_93ac73'

def setup_inputs(seed: int = 0):
    np.random.seed(seed)
    _w = jnp.asarray
    def _rec_inputs():
        import jax
        import jax.numpy as jnp
        _gk = jax.random.key(seed)
        x = -0.000357 + 1 * jax.random.normal(jax.random.fold_in(_gk, 1), (32, 56, 56, 192), jnp.float32)
        return x
    x = _rec_inputs()
    def _L0_conv_setup():
        import jax, jax.numpy as jnp
        import numpy as np
        WIN = 7
        SHIFT = 3
        HEADS = 6

        def _rel_position_index():
            ch = np.arange(WIN)
            coords = np.stack(np.meshgrid(ch, ch, indexing='ij')).reshape(2, -1)
            rel = coords[:, :, None] - coords[:, None, :]
            rel = rel.transpose(1, 2, 0).copy()
            rel[:, :, 0] += WIN - 1
            rel[:, :, 1] += WIN - 1
            rel[:, :, 0] *= 2 * WIN - 1
            return rel.sum(-1).reshape(-1)

        def _shift_mask(pH, pW):
            m = np.zeros((pH, pW), dtype=np.float32)
            h_slices = ((0, pH - WIN), (pH - WIN, pH - SHIFT), (pH - SHIFT, pH))
            w_slices = ((0, pW - WIN), (pW - WIN, pW - SHIFT), (pW - SHIFT, pW))
            count = 0
            for h0, h1 in h_slices:
                for w0, w1 in w_slices:
                    m[h0:h1, w0:w1] = count
                    count += 1
            nWh, nWw = (pH // WIN, pW // WIN)
            m = m.reshape(nWh, WIN, nWw, WIN).transpose(0, 2, 1, 3).reshape(-1, WIN * WIN)
            diff = m[:, None, :] - m[:, :, None]
            return np.where(diff != 0, np.float32(-100.0), np.float32(0.0))
        REL_INDEX = _rel_position_index()
        key = jax.random.key(seed)
        ks = jax.random.split(key, 6)
        B, H, W, C = (32, 56, 56, 192)
        return {'x': jax.random.normal(ks[0], (B, H, W, C), dtype=jnp.float32), 'qkv_weight': jax.random.normal(ks[1], (3 * C, C), dtype=jnp.float32) * 0.02, 'qkv_bias': jax.random.normal(ks[2], (3 * C,), dtype=jnp.float32) * 0.02, 'proj_weight': jax.random.normal(ks[3], (C, C), dtype=jnp.float32) * 0.02, 'proj_bias': jax.random.normal(ks[4], (C,), dtype=jnp.float32) * 0.02, 'rel_bias_table': jax.random.normal(ks[5], ((2 * WIN - 1) ** 2, HEADS), dtype=jnp.float32) * 0.02}
    _L0_conv_all = _L0_conv_setup()
    _L0_conv_in = {k: v for k, v in _L0_conv_all.items() if k in ('qkv_weight', 'qkv_bias', 'proj_weight', 'proj_bias', 'rel_bias_table', )}
    del _L0_conv_all

    def _L1_conv_setup():
        import jax, jax.numpy as jnp
        import numpy as np
        DIM = 192
        HEADS = 6
        HEAD_DIM = DIM // HEADS
        K = 3
        PAD = 1
        STRIDE = 2
        SCALE = HEAD_DIM ** (-0.5)
        B, H, W = (16, 56, 56)
        key = jax.random.key(seed)
        ks = jax.random.split(key, 6)
        x = jax.random.normal(ks[0], (B, H, W, DIM), jnp.float32)
        Wv = jax.random.normal(ks[1], (DIM, DIM), jnp.float32) * 0.05
        Wa = jax.random.normal(ks[2], (DIM, K ** 4 * HEADS), jnp.float32) * 0.05
        ba = jax.random.normal(ks[3], (K ** 4 * HEADS,), jnp.float32) * 0.01
        Wp = jax.random.normal(ks[4], (DIM, DIM), jnp.float32) * 0.05
        bp = jax.random.normal(ks[5], (DIM,), jnp.float32) * 0.01
        return {'x': x, 'Wv': Wv, 'Wa': Wa, 'ba': ba, 'Wp': Wp, 'bp': bp}
    _L1_conv_all = _L1_conv_setup()
    _L1_conv_in = {k: v for k, v in _L1_conv_all.items() if k in ('Wv', 'Wa', 'ba', 'Wp', 'bp', )}
    del _L1_conv_all

    return {
        "x": x,
        "L0_conv_qkv_weight": _L0_conv_in["qkv_weight"],
        "L0_conv_qkv_bias": _L0_conv_in["qkv_bias"],
        "L0_conv_proj_weight": _L0_conv_in["proj_weight"],
        "L0_conv_proj_bias": _L0_conv_in["proj_bias"],
        "L0_conv_rel_bias_table": _L0_conv_in["rel_bias_table"],
        "L1_conv_Wv": _L1_conv_in["Wv"],
        "L1_conv_Wa": _L1_conv_in["Wa"],
        "L1_conv_ba": _L1_conv_in["ba"],
        "L1_conv_Wp": _L1_conv_in["Wp"],
        "L1_conv_bp": _L1_conv_in["bp"],
    }

def reference(x, L0_conv_qkv_weight, L0_conv_qkv_bias, L0_conv_proj_weight, L0_conv_proj_bias, L0_conv_rel_bias_table, L1_conv_Wv, L1_conv_Wa, L1_conv_ba, L1_conv_Wp, L1_conv_bp):
    import jax
    import jax.numpy as jnp
    def _L0_conv_ref(x, qkv_weight, qkv_bias, proj_weight, proj_bias, rel_bias_table):
        import jax, jax.numpy as jnp
        import numpy as np
        WIN = 7
        SHIFT = 3
        HEADS = 6

        def _rel_position_index():
            ch = np.arange(WIN)
            coords = np.stack(np.meshgrid(ch, ch, indexing='ij')).reshape(2, -1)
            rel = coords[:, :, None] - coords[:, None, :]
            rel = rel.transpose(1, 2, 0).copy()
            rel[:, :, 0] += WIN - 1
            rel[:, :, 1] += WIN - 1
            rel[:, :, 0] *= 2 * WIN - 1
            return rel.sum(-1).reshape(-1)

        def _shift_mask(pH, pW):
            m = np.zeros((pH, pW), dtype=np.float32)
            h_slices = ((0, pH - WIN), (pH - WIN, pH - SHIFT), (pH - SHIFT, pH))
            w_slices = ((0, pW - WIN), (pW - WIN, pW - SHIFT), (pW - SHIFT, pW))
            count = 0
            for h0, h1 in h_slices:
                for w0, w1 in w_slices:
                    m[h0:h1, w0:w1] = count
                    count += 1
            nWh, nWw = (pH // WIN, pW // WIN)
            m = m.reshape(nWh, WIN, nWw, WIN).transpose(0, 2, 1, 3).reshape(-1, WIN * WIN)
            diff = m[:, None, :] - m[:, :, None]
            return np.where(diff != 0, np.float32(-100.0), np.float32(0.0))
        REL_INDEX = _rel_position_index()
        B, H, W, C = x.shape
        head_dim = C // HEADS
        N = WIN * WIN
        pad_b = (WIN - H % WIN) % WIN
        pad_r = (WIN - W % WIN) % WIN
        x = jnp.pad(x, ((0, 0), (0, pad_b), (0, pad_r), (0, 0)))
        pH, pW = (H + pad_b, W + pad_r)
        sh = [SHIFT if WIN < pH else 0, SHIFT if WIN < pW else 0]
        shifted = sh[0] + sh[1] > 0
        if shifted:
            x = jnp.roll(x, (-sh[0], -sh[1]), axis=(1, 2))
        nWh, nWw = (pH // WIN, pW // WIN)
        nW = nWh * nWw
        xw = x.reshape(B, nWh, WIN, nWw, WIN, C).transpose(0, 1, 3, 2, 4, 5).reshape(B * nW, N, C)
        qkv = xw @ qkv_weight.T + qkv_bias
        qkv = qkv.reshape(B * nW, N, 3, HEADS, head_dim).transpose(2, 0, 3, 1, 4)
        q, k, v = (qkv[0], qkv[1], qkv[2])
        q = q * head_dim ** (-0.5)
        attn = jnp.einsum('whnd,whmd->whnm', q, k)
        rel_bias = rel_bias_table[REL_INDEX].reshape(N, N, HEADS).transpose(2, 0, 1)
        attn = attn + rel_bias[None]
        if shifted:
            mask = jnp.asarray(_shift_mask(pH, pW))
            attn = attn.reshape(B, nW, HEADS, N, N) + mask[None, :, None]
            attn = attn.reshape(B * nW, HEADS, N, N)
        attn = jax.nn.softmax(attn, axis=-1)
        out = jnp.einsum('whnm,whmd->whnd', attn, v)
        out = out.transpose(0, 2, 1, 3).reshape(B * nW, N, C)
        out = out @ proj_weight.T + proj_bias
        out = out.reshape(B, nWh, nWw, WIN, WIN, C).transpose(0, 1, 3, 2, 4, 5).reshape(B, pH, pW, C)
        if shifted:
            out = jnp.roll(out, (sh[0], sh[1]), axis=(1, 2))
        return out[:, :H, :W, :]

    def _L1_conv_ref(x, Wv, Wa, ba, Wp, bp):
        import jax, jax.numpy as jnp
        import numpy as np
        DIM = 192
        HEADS = 6
        HEAD_DIM = DIM // HEADS
        K = 3
        PAD = 1
        STRIDE = 2
        SCALE = HEAD_DIM ** (-0.5)
        B, H, W = (16, 56, 56)
        Bn, Hn, Wn, C = x.shape
        h = -(-Hn // STRIDE)
        w = -(-Wn // STRIDE)
        KK = K * K
        v = x @ Wv
        vp = jnp.pad(v, ((0, 0), (PAD, PAD), (PAD, PAD), (0, 0)))
        patches = jnp.stack([vp[:, i:i + STRIDE * h:STRIDE, j:j + STRIDE * w:STRIDE, :] for i in range(K) for j in range(K)], axis=3)
        patches = patches.reshape(Bn, h * w, KK, HEADS, HEAD_DIM)
        pooled = x.reshape(Bn, h, STRIDE, w, STRIDE, C).mean(axis=(2, 4))
        a = pooled.reshape(Bn, h * w, C) @ Wa + ba
        a = a.reshape(Bn, h * w, HEADS, KK, KK) * SCALE
        a = jax.nn.softmax(a, axis=-1)
        out = jnp.einsum('bnhpq,bnqhd->bnphd', a, patches)
        out = out.reshape(Bn, h, w, KK, C)
        acc = jnp.zeros((Bn, Hn + 2 * PAD, Wn + 2 * PAD, C), x.dtype)
        idx = 0
        for i in range(K):
            for j in range(K):
                acc = acc.at[:, i:i + STRIDE * h:STRIDE, j:j + STRIDE * w:STRIDE, :].add(out[:, :, :, idx, :])
                idx += 1
        y = acc[:, PAD:PAD + Hn, PAD:PAD + Wn, :]
        return y @ Wp + bp

    def _gn(v, G=32, eps=1e-5):
        B_, H_, W_, C_ = v.shape
        g = v.reshape(B_, H_, W_, G, C_ // G)
        m = jnp.mean(g, axis=(1, 2, 4), keepdims=True)
        s = jnp.var(g, axis=(1, 2, 4), keepdims=True)
        return ((g - m) / jnp.sqrt(s + eps)).reshape(v.shape)

    def _ln_c(v, eps=1e-6):
        m = jnp.mean(v, axis=-1, keepdims=True)
        s = jnp.var(v, axis=-1, keepdims=True)
        return (v - m) / jnp.sqrt(s + eps)

    def _ln_t(v, eps=1e-5):
        m = jnp.mean(v, axis=-1, keepdims=True)
        s = jnp.var(v, axis=-1, keepdims=True)
        return (v - m) / jnp.sqrt(s + eps)

    def _to_tokens(v):
        B_, H_, W_, C_ = v.shape
        return v.reshape(B_, H_ * W_, C_)
    def _from_tokens(t, like):
        return t.reshape(like.shape)

    x = x + _L0_conv_ref(_gn(x), L0_conv_qkv_weight, L0_conv_qkv_bias, L0_conv_proj_weight, L0_conv_proj_bias, L0_conv_rel_bias_table)
    x = x + _L1_conv_ref(_gn(x), L1_conv_Wv, L1_conv_Wa, L1_conv_ba, L1_conv_Wp, L1_conv_bp)
    return x


_drawn_inputs = setup_inputs


def setup_inputs(seed=0):
    import zlib

    import numpy as np

    out = dict(_drawn_inputs(seed))
    spreads = {}
    factors = {'L0_conv_qkv_weight': 3.592,
     'L0_conv_qkv_bias': 8.0,
     'L0_conv_proj_weight': 3.165,
     'L0_conv_rel_bias_table': 8.0,
     'L1_conv_Wa': 4.302,
     'L1_conv_ba': 64.0,
     'L1_conv_bp': 5.531}
    for name, (base, spread) in spreads.items():
        noise = np.random.default_rng([zlib.crc32(name.encode()), seed]).standard_normal(out[name].shape)
        drawn = base * np.exp(spread * noise) if base else spread * noise
        out[name] = jnp.asarray(drawn.astype(out[name].dtype))
    for name, factor in factors.items():
        out[name] = (out[name] * factor).astype(out[name].dtype)
    return out
```

```python
from contextlib import ExitStack

import numpy as np
import concourse.bass as bass
from concourse import mybir

F32 = mybir.dt.float32
ALU = mybir.AluOpType
ACT = mybir.ActivationFunctionType
AX = mybir.AxisListType

B, H, W, C = 32, 56, 56, 192
HEADS, HD = 6, 32
WIN, SHIFT = 7, 3
NTOK = WIN * WIN
NWIN = H // WIN
ROW = NWIN * NTOK
CH = 96
NC = C // CH
HC = HEADS // NC
GROUPS = 32
GC = C // GROUPS
GN_EPS = 1e-5
PADW = 64
PAIRS = NWIN // 2
QSCALE = HD ** -0.5
LOGIT = HC * NTOK
K = 3
KK = K * K
HN = H // 2
HALF = HN // 2
SX = 32
IP = 32
RAS = 60
PJ = KK * HALF
AH = HC * KK * KK
BN = 6
STAT_STEPS = 16 + 2 + 4 + 3


def at(eng, sem, value):
    if isinstance(value, int) and value <= 0:
        return
    eng.wait_ge(sem, value)




def past(eng, sem, value):
    at(eng, sem, value + 1)


def start_at_one(eng, *sems):
    for s in sems:
        eng.sem_inc(s, 1)


class Stats:

    def __init__(self, sb, sem, tag, psum, gmat, x_row, passed):
        self.bn = sb("bn_" + tag, [CH, NC, NWIN, BN])
        self.mv = sb("mv_" + tag, [CH, NC, 2])
        self.dev = sb("dev_" + tag, [CH, NC])
        self.gmean = sb("gmean_" + tag, [CH, NC])
        self.norm = sb("norm_" + tag, [CH, 2, 2, NC])
        self.var = sb("var_" + tag, [CH, NC])
        self.std = sb("std_" + tag, [CH, NC])
        self.rooted = sem("rooted_" + tag)
        self.passed = passed
        self.step = sem("stat_step_" + tag)
        self.mm = sem("stat_mm_" + tag)
        self.psum, self.gmat, self.x_row = psum, gmat, x_row

    def rows(self, dve, i, rows):
        for row in rows:
            for c in range(NC):
                dve.bn_stats(self.bn[:, c, row, :], self.x_row(i, row, c)).then_inc(self.step, 1)

    def aggregate(self, dve, i):
        dve.wait_ge(self.step, i * STAT_STEPS + 16)
        dve.sem_inc(self.passed, 1)
        for c in range(NC):
            dve.bn_aggr(self.mv[:, c, :], self.bn[:, c, :, :].rearrange("p a b -> p (a b)")) \
                .then_inc(self.step, 1)

    def mean_mm(self, pe, i):
        pe.wait_ge(self.step, i * STAT_STEPS + 18)
        pe.matmul(self.psum[:, 0:NC], self.gmat[:, :], self.mv[:, :, 0], start=True, stop=True) \
            .then_inc(self.mm, 1)

    def spread(self, dve, i):
        dve.wait_ge(self.mm, 2 * i + 1)
        dve.tensor_tensor(self.dev[:, :], self.mv[:, :, 0], self.psum[:, 0:NC], ALU.subtract) \
            .then_inc(self.step, 1)
        dve.tensor_copy(self.gmean[:, :], self.psum[:, 0:NC]).then_inc(self.step, 1)
        dve.wait_ge(self.step, i * STAT_STEPS + 20)
        dve.tensor_tensor(self.dev[:, :], self.dev[:, :], self.dev[:, :], ALU.mult) \
            .then_inc(self.step, 1)
        dve.wait_ge(self.step, i * STAT_STEPS + 21)
        dve.tensor_tensor(self.dev[:, :], self.dev[:, :], self.mv[:, :, 1], ALU.add) \
            .then_inc(self.step, 1)

    def var_mm(self, pe, i):
        pe.wait_ge(self.step, i * STAT_STEPS + 22)
        pe.matmul(self.psum[:, 0:NC], self.gmat[:, :], self.dev[:, :], start=True, stop=True) \
            .then_inc(self.mm, 1)

    def variance(self, dve, i):
        dve.wait_ge(self.mm, 2 * i + 2)
        dve.tensor_scalar(self.var[:, :], self.psum[:, 0:NC], GN_EPS, None, ALU.add).then_inc(self.step, 1)

    def root(self, act, i):
        act.wait_ge(self.step, i * STAT_STEPS + 23)
        act.activation(self.std[:, :], self.var[:, :], ACT.Sqrt).then_inc(self.rooted, 1)

    def affine(self, dve, i):
        scale = self.norm[:, bass.ds(i % 2, 1), 0, :].rearrange("p a c -> p (a c)")
        bias = self.norm[:, bass.ds(i % 2, 1), 1, :].rearrange("p a c -> p (a c)")
        dve.wait_ge(self.rooted, i + 1)
        dve.reciprocal(scale, self.std[:, :]).then_inc(self.step, 1)
        dve.wait_ge(self.step, i * STAT_STEPS + 24)
        dve.scalar_tensor_tensor(out=bias, in0=self.gmean[:, :], scalar=-1.0, in1=scale,
                                 op0=ALU.mult, op1=ALU.mult).then_inc(self.step, 1)

    def affine_of(self, i, c):
        return (self.norm[:, bass.ds(i % 2, 1), 0, c], self.norm[:, bass.ds(i % 2, 1), 1, c])


def window_layer(nc, x_in, x1, w_qkv, b_qk, b_v, w_proj, b_proj, rel, mask, gmat_d, kmask_d, ident_d):
    with ExitStack() as ctx:
        def sb(name, shape):
            return ctx.enter_context(nc.sbuf_tensor(name, shape, F32))

        def sem(name):
            return ctx.enter_context(nc.semaphore(name))

        bank = [ctx.enter_context(nc.psum_tensor(f"l0_bank{i}", [128, 512], F32)) for i in range(8)]
        QK, VB, PT, OB = bank[0:2], bank[2], bank[5:7], bank[7]
        s_ctx = bank[3:5]

        x = sb("x", [CH, 2 * NWIN, NC, ROW])
        wqkv = sb("wqkv", [CH, NC, 3 * C])
        wp_sb = sb("wp_sb", [128, 2, C])
        bqk = sb("bqk", [CH, 4])
        bqs = sb("bqs", [CH, NC])
        bv = sb("bv", [128, 2])
        bp = sb("bp", [CH, NC])
        gmat = sb("gmat", [CH, CH])
        kmask = sb("kmask", [CH, HC])
        ident = sb("ident", [128, 128])
        rel_sb = sb("rel_sb", [128, HEADS, NTOK])
        mask_sb = sb("mask_sb", [128, 2, PAIRS, NTOK])
        bias = sb("bias", [128, 2, PAIRS, HEADS, NTOK])
        xn = sb("xn", [CH, 2, NC, NWIN, PADW])
        q = sb("q", [CH, 2, NC, NWIN, PADW])
        kbd = sb("kbd", [CH, 2, NC, HC, ROW])
        vbd = sb("vbd", [128, 2, NWIN, 3, 2 * HD])
        logit = sb("logit", [128, PAIRS, HEADS, NTOK])
        prob = sb("prob", [128, 2, PAIRS, HEADS, PADW])
        top = sb("top", [128, PAIRS * HEADS])
        total = sb("total", [128, PAIRS * HEADS])
        rtotal = sb("rtotal", [128, PAIRS * HEADS])
        pt = sb("pt", [128, 2, 3, 128])
        o = sb("o", [128, 2, 2, ROW])

        consts = sem("consts")
        zeroed = sem("zeroed")
        bias_ready = sem("bias_ready")
        x_loaded = sem("x_loaded")
        x_stored = sem("x_stored")
        xn_ready = sem("xn_ready")
        q_raw, q_ready = sem("q_raw"), sem("q_ready")
        k_raw, k_ready = sem("k_raw"), sem("k_ready")
        v_raw, v_ready = sem("v_raw"), sem("v_ready")
        s_raw, s_biased = sem("s_raw"), sem("s_biased")
        top_ready, centred = sem("top_ready"), sem("centred")
        exp_ready, total_ready, rtotal_ready = sem("exp_ready"), sem("total_ready"), sem("rtotal_ready")
        prob_ready = sem("prob_ready")
        pt_raw, pt_ready = sem("pt_raw"), sem("pt_ready")
        pv_done = sem("pv_done")
        o_raw, o_ready = sem("o_raw"), sem("o_ready")
        proj_raw, res_done = sem("proj_raw"), sem("res_done")

        NCONST = 11
        stats = Stats(sb, sem, "l0", OB[0:CH, :], gmat,
                      lambda i, row, c: x[:, bass.ds((i * NWIN + row) % (2 * NWIN), 1), c, :]
                      .rearrange("p a n -> p (a n)"), sem("passed"))

        def x_row(r, c):
            return x[:, bass.ds(r % (2 * NWIN), 1), c, :].rearrange("p a (w n) -> p (a w) n", n=NTOK)


        def act_norm(act, r, i, s):
            at(act, stats.step, (i + 1) * STAT_STEPS)
            at(act, v_raw, 2 * (r - 1))
            for c in range(NC):
                scale, shift = stats.affine_of(i, c)
                act.activation(xn[:, s, c, :, 0:NTOK], x_row(r, c), ACT.Identity, bias=shift,
                               scale=scale).then_inc(xn_ready, 1)

        def pe_qk(pe, r, s, which):
            pe.wait_ge(xn_ready, 2 * (r + 1))
            for c in range(NC):
                if which == 0:
                    past(pe, res_done, 2 * (r - 1))
                else:
                    pe.wait_ge(q_ready, 2 * r + c + 1)
                for kc in range(NC):
                    mm = pe.matmul(QK[c][0:CH, 0:ROW], wqkv[:, kc, which * C + c * CH:which * C + (c + 1) * CH],
                                   xn[:, s, kc, :, 0:NTOK], start=(kc == 0), stop=(kc == NC - 1))
                mm.then_inc(k_raw if which else q_raw, 1)

        def act_q(act, r, s):
            past(act, s_raw, 2 * (r - 1))
            for c in range(NC):
                act.wait_ge(q_raw, 2 * r + c + 1)
                act.activation(q[:, s, c, :, 0:NTOK],
                               QK[c][0:CH, 0:ROW].rearrange("p (w n) -> p w n", n=NTOK), ACT.Identity,
                               bias=bqs[:, c:c + 1], scale=QSCALE).then_inc(q_ready, 1)

        def dve_k(dve, r, s):
            past(dve, s_raw, 2 * (r - 1))
            for c in range(NC):
                dve.wait_ge(k_raw, 2 * r + c + 1)
                dve.scalar_tensor_tensor(
                    out=kbd[:, s, c, :, :],
                    in0=QK[c][0:CH, 0:ROW].unsqueeze(1).broadcast_to([CH, HC, ROW]),
                    scalar=bqk[:, 2 + c:3 + c],
                    in1=kmask[:, :].unsqueeze(2).broadcast_to([CH, HC, ROW]),
                    op0=ALU.add, op1=ALU.mult).then_inc(k_ready, 1)

        def pe_v(pe, r, s):
            for half in range(2):
                at(pe, v_ready, 2 * r + half)
                for p in range(2):
                    for kc in range(NC):
                        mm = pe.matmul(VB[:, p * C:(p + 1) * C],
                                       xn[:, s, kc, 4 * half + 2 * p:4 * half + 2 * p + 2, :]
                                       .rearrange("p w n -> p (w n)"),
                                       wqkv[:, kc, 2 * C:3 * C], start=(kc == 0), stop=(kc == NC - 1))
                mm.then_inc(v_raw, 1)

        def dve_v(dve, r, s):
            past(dve, pv_done, 4 * (r - 1))
            for half in range(2):
                dve.wait_ge(v_raw, 2 * r + half + 1)
                for w in range(2):
                    for odd in range(2):
                        src = VB[64 * w:64 * w + 64, 0:2 * C].rearrange(
                            "p (a h o d) -> p a h o d", a=2, h=3, o=2)[:, :, :, odd, :]
                        dst = vbd[64 * odd:64 * odd + 64, s, 4 * half + w:4 * half + w + 3:2, :,
                                  odd * HD:(odd + 1) * HD]
                        cp = dve.tensor_copy(dst, src)
                cp.then_inc(v_ready, 1)

        def pe_logits(pe, r, s):
            pe.wait_ge(k_ready, 2 * (r + 1))
            for half in range(2):
                at(pe, s_biased, 2 * r + half)
                for p in range(2):
                    for w in range(2):
                        win = 4 * half + 2 * p + w
                        for c in range(NC):
                            mm = pe.matmul(s_ctx[p][64 * w:64 * w + 64, c * LOGIT:(c + 1) * LOGIT],
                                           q[:, s, c, win, :],
                                           kbd[:, s, c, :, win * NTOK:(win + 1) * NTOK],
                                           start=True, stop=True)
                mm.then_inc(s_raw, 1)

        def dve_softmax_top(dve, r, last_row):
            for half in range(2):
                past(dve, s_raw, 2 * r + half + 1)
                at(dve, exp_ready, r)
                for p in range(2):
                    add = dve.tensor_tensor(
                        logit[:, 2 * half + p, :, :].rearrange("p h m -> p (h m)"),
                        s_ctx[p][:, 0:2 * LOGIT],
                        bias[:, last_row, 2 * half + p, :, :].rearrange("p h m -> p (h m)"), ALU.add)
                add.then_inc(s_biased, 1)
            dve.wait_ge(s_biased, 2 * (r + 1))
            dve.tensor_reduce(top[:, :], logit[:, :, :, :].rearrange("p a h m -> p (a h) m"),
                              AX.X, ALU.max).then_inc(top_ready, 1)

        def pool_centre(pool, r):
            pool.wait_ge(top_ready, r + 1)
            lg = logit[:, :, :, :].rearrange("p a h m -> p (a h) m")
            pool.tensor_tensor(lg, lg, top[:, :].unsqueeze(2).broadcast_to([128, PAIRS * HEADS, NTOK]),
                               ALU.subtract).then_inc(centred, 1)

        def act_exp(act, r, s):
            act.wait_ge(centred, r + 1)
            past(act, pt_raw, 4 * (r - 1))
            act.activation(prob[:, s, :, :, 0:NTOK].rearrange("p a h m -> p (a h) m"),
                           logit[:, :, :, :].rearrange("p a h m -> p (a h) m"), ACT.Exp) \
                .then_inc(exp_ready, 1)

        def dve_total(dve, r, s):
            dve.wait_ge(exp_ready, r + 1)
            at(dve, prob_ready, r)
            dve.tensor_reduce(total[:, :], prob[:, s, :, :, 0:NTOK].rearrange("p a h m -> p (a h) m"),
                              AX.X, ALU.add).then_inc(total_ready, 1)
            dve.wait_ge(total_ready, r + 1)
            dve.reciprocal(rtotal[:, :], total[:, :]).then_inc(rtotal_ready, 1)

        def pool_scale(pool, r, s):
            pool.wait_ge(rtotal_ready, r + 1)
            pr = prob[:, s, :, :, 0:NTOK].rearrange("p a h m -> p (a h) m")
            pool.tensor_tensor(pr, pr, rtotal[:, :].unsqueeze(2).broadcast_to([128, PAIRS * HEADS, NTOK]),
                               ALU.mult).then_inc(prob_ready, 1)

        def pe_attend(pe, r, s):
            pe.wait_ge(prob_ready, r + 1)

            def turn(p):
                past(pe, pt_ready, 4 * r + max(p - 1, 0))
                for hp in range(3):
                    mm = pe.transpose(PT[p % 2][:, hp * 128:(hp + 1) * 128],
                                      prob[:, s, p, 2 * hp:2 * hp + 2, :].rearrange("p h m -> p (h m)"),
                                      ident[:, :])
                mm.then_inc(pt_raw, 1)

            def attend(p):
                past(pe, pt_ready, 4 * r + p + 1)
                if p % 2 == 0:
                    past(pe, o_ready, 2 * r + p // 2)
                    if p == 0:
                        pe.wait_ge(v_ready, 2 * (r + 1))
                for w in range(2):
                    col = (2 * (p % 2) + w) * NTOK
                    for hp in range(3):
                        rows = 64 * (hp % 2)
                        cols = col + (hp // 2) * (ROW // 2)
                        mm = pe.matmul(OB[rows:rows + 64, cols:cols + NTOK], vbd[:, s, 2 * p + w, hp, :],
                                       pt[:, p % 2, hp, 64 * w:64 * w + NTOK], start=True, stop=True)
                mm.then_inc(pv_done, 1)

            turn(0)
            for p in range(PAIRS):
                if p + 1 < PAIRS:
                    turn(p + 1)
                attend(p)

        def act_attend(act, r, s):
            for p in range(PAIRS):
                past(act, pt_raw, 4 * r + p + 1)
                past(act, pv_done, 4 * r + max(p - 1, 0))
                act.activation(pt[:, p % 2, :, :].rearrange("p h n -> p (h n)"), PT[p % 2][:, 0:384],
                               ACT.Copy).then_inc(pt_ready, 1)
                if p % 2 == 1:
                    half = p // 2
                    past(act, pv_done, 4 * r + p + 1)
                    lo, hi = half * (ROW // 2), (half + 1) * (ROW // 2)
                    act.activation(o[:, s, 0, lo:hi], OB[:, 0:ROW // 2], ACT.Identity, bias=bv[:, 0:1])
                    act.activation(o[0:64, s, 1, lo:hi], OB[0:64, ROW // 2:ROW], ACT.Identity,
                                   bias=bv[0:64, 1:2]).then_inc(o_ready, 1)

        def pe_proj(pe, r, s, k_after):
            past(pe, o_ready, 2 * (r + 1))
            for c in range(NC):
                if k_after:
                    pe.wait_ge(k_ready, 2 * (r + 1) + c + 1)
                else:
                    past(pe, res_done, 2 * r)
                pe.matmul(QK[c][0:CH, 0:ROW], wp_sb[:, 0, c * CH:(c + 1) * CH], o[:, s, 0, :],
                          start=True, stop=False)
                pe.matmul(QK[c][0:CH, 0:ROW], wp_sb[0:64, 1, c * CH:(c + 1) * CH], o[0:64, s, 1, :],
                          start=False, stop=True).then_inc(proj_raw, 1)

        def dve_residual(dve, r):
            for c in range(NC):
                dve.wait_ge(proj_raw, 2 * r + c + 1)
                row = x[:, bass.ds(r % (2 * NWIN), 1), c, :].rearrange("p a n -> p (a n)")
                dve.scalar_tensor_tensor(out=row, in0=QK[c][0:CH, 0:ROW], scalar=bp[:, c:c + 1], in1=row,
                                         op0=ALU.add, op1=ALU.add).then_inc(res_done, 1)


        def pe_front(pe, r, s):
            pe_qk(pe, r, s, 0)
            pe_qk(pe, r, s, 1)
            pe_v(pe, r, s)
            pe_logits(pe, r, s)

        def dve_front(dve, r, s, last_row):
            dve_k(dve, r, s)
            dve_v(dve, r, s)
            dve_softmax_top(dve, r, last_row)
            dve_total(dve, r, s)

        block = ctx.enter_context(nc.Block())

        @block.sync
        def _(sp):
            for src, dst in ((w_qkv, wqkv[:, :, :]), (w_proj[0:128, :], wp_sb[:, 0, :]),
                             (w_proj[128:192, :], wp_sb[0:64, 1, :]), (b_qk, bqk[:, :]), (b_v, bv[:, :]),
                             (b_proj, bp[:, :]), (gmat_d, gmat[:, :]), (kmask_d, kmask[:, :]),
                             (ident_d, ident[:, :]), (rel, rel_sb[:, :, :]), (mask, mask_sb[:, :, :, :])):
                sp.dma_start(dst, src).then_inc(consts, 16)

            def load(i, slot):
                sp.dma_start(x[:, slot * NWIN:(slot + 1) * NWIN, :, :].rearrange("p a c n -> p (a c n)"),
                             x_in[bass.ds(i, 1), :, :].rearrange("a p n -> (a p) n")).then_inc(x_loaded, 16)

            def store(i, slot):
                past(sp, res_done, 2 * NWIN * (i + 1))
                sp.dma_start(x1[bass.ds(i, 1), :, :].rearrange("a p n -> (a p) n"),
                             x[:, slot * NWIN:(slot + 1) * NWIN, :, :].rearrange("p a c n -> p (a c n)")) \
                    .then_inc(x_stored, 16)
                sp.wait_ge(x_stored, 16 * (i + 1))

            load(0, 0)
            sp.wait_ge(x_loaded, 16)
            load(1, 1)
            with sp.Fori(0, B // 2 - 1) as pair:
                for slot in range(2):
                    store(2 * pair + slot, slot)
                    sp.wait_ge(x_loaded, 16 * (2 * pair + slot + 2))
                    load(2 * pair + slot + 2, slot)
            for slot in range(2):
                store(B - 2 + slot, slot)

        @block.gpsimd
        def _(pool):
            start_at_one(pool, res_done, s_raw, pv_done, pt_raw, pt_ready, o_ready)
            for t in (xn[:, :, :, :, NTOK:PADW], q[:, :, :, :, NTOK:PADW], prob[:, :, :, :, NTOK:PADW],
                      vbd[:, :, :, :, :]):
                pool.memset(t, 0.0).then_inc(zeroed, 1)
            def row(r, s):
                pool_centre(pool, r)
                pool_scale(pool, r, s)

            row(0, 0)

            def image(i, last):
                with pool.Fori(0, 3) as p:
                    row(i * NWIN + 2 * p + 1, 1)
                    row(i * NWIN + 2 * p + 2, 0)
                row(i * NWIN + 7, 1)
                if not last:
                    row(i * NWIN + 8, 0)

            with pool.Fori(0, B - 1) as i:
                image(i, False)
            image(B - 1, True)

        @block.vector
        def _(dve):
            dve.wait_ge(consts, 16 * NCONST)
            dve.tensor_scalar(bqs[:, :], bqk[:, 0:NC], QSCALE, None, ALU.mult).then_inc(bias_ready, 1)
            for last_row in range(2):
                for p in range(PAIRS):
                    dve.tensor_tensor(bias[:, last_row, p, :, :], rel_sb[:, :, :],
                                      mask_sb[:, last_row, p, :].unsqueeze(1)
                                      .broadcast_to([128, HEADS, NTOK]), ALU.add).then_inc(bias_ready, 1)
            dve.wait_ge(bias_ready, 9)
            dve.wait_ge(zeroed, 4)
            dve.wait_ge(x_loaded, 16)
            stats.rows(dve, 0, range(NWIN))
            stats.aggregate(dve, 0)
            stats.spread(dve, 0)
            stats.variance(dve, 0)
            stats.affine(dve, 0)
            dve_front(dve, 0, 0, 0)

            def image(i, last):
                if not last:
                    dve.wait_ge(x_loaded, 16 * (i + 2))
                    stats.rows(dve, i + 1, range(NWIN))
                    stats.aggregate(dve, i + 1)

                def pair(j0, last_pair=False):
                    for k in range(2):
                        r = i * NWIN + j0 + k
                        if not (last and last_pair and k == 1):
                            dve_front(dve, r + 1, (k + 1) % 2, int(last_pair and k == 0))
                        dve_residual(dve, r)

                with dve.Fori(0, 2) as p:
                    pair(2 * p)
                if not last:
                    stats.spread(dve, i + 1)
                pair(4)
                if not last:
                    stats.variance(dve, i + 1)
                    stats.affine(dve, i + 1)
                pair(6, True)

            with dve.Fori(0, B - 1) as i:
                image(i, False)
            image(B - 1, True)

        @block.scalar
        def _(act):
            act.wait_ge(zeroed, 4)
            act.wait_ge(bias_ready, 9)
            act.wait_ge(x_loaded, 16)
            stats.root(act, 0)
            act_norm(act, 0, 0, 0)
            act_norm(act, 1, 0, 1)
            act_q(act, 0, 0)
            act_exp(act, 0, 0)

            def image(i, last):
                def pair(j0, last_pair=False):
                    for k in range(2):
                        r = i * NWIN + j0 + k
                        if not (last and last_pair):
                            act_norm(act, r + 2, i + 1 if last_pair else i, k)
                        if not (last and last_pair and k == 1):
                            act_q(act, r + 1, (k + 1) % 2)
                        act_attend(act, r, k)
                        if not (last and last_pair and k == 1):
                            act_exp(act, r + 1, (k + 1) % 2)

                with act.Fori(0, 3) as p:
                    pair(2 * p)
                if not last:
                    stats.root(act, i + 1)
                    act.wait_ge(x_loaded, 16 * (i + 2))
                pair(6, True)

            with act.Fori(0, B - 1) as i:
                image(i, False)
            image(B - 1, True)

        @block.tensor
        def _(pe):
            pe.wait_ge(consts, 16 * NCONST)
            pe.wait_ge(zeroed, 4)
            stats.mean_mm(pe, 0)
            stats.var_mm(pe, 0)
            pe_front(pe, 0, 0)

            def image(i, last):
                def pair(j0, last_pair=False):
                    for k in range(2):
                        r = i * NWIN + j0 + k
                        more = not (last and last_pair and k == 1)
                        if more:
                            pe_front(pe, r + 1, (k + 1) % 2)
                        pe_attend(pe, r, k)
                        pe_proj(pe, r, k, more)

                with pe.Fori(0, 2) as p:
                    pair(2 * p)
                if not last:
                    stats.mean_mm(pe, i + 1)
                    pe.wait_ge(stats.step, (i + 1) * STAT_STEPS + 20)
                pair(4)
                if not last:
                    stats.var_mm(pe, i + 1)
                    pe.wait_ge(stats.step, (i + 1) * STAT_STEPS + 23)
                pair(6, True)

            with pe.Fori(0, B - 1) as i:
                image(i, False)
            image(B - 1, True)


def outlook_layer(nc, x1, out, w_v, w_a, b_a, w_proj, b_proj, gmat_d):
    with ExitStack() as ctx:
        def sb(name, shape):
            return ctx.enter_context(nc.sbuf_tensor(name, shape, F32))

        def sem(name):
            return ctx.enter_context(nc.semaphore(name))

        bank = [ctx.enter_context(nc.psum_tensor(f"l1_bank{i}", [128, 512], F32)) for i in range(8)]
        VB = bank[7]
        IB = 4
        NB = HN // IB
        NG = NC * 2
        NH = NG * HC

        x = sb("x1_sb", [CH, NWIN, NC, ROW])
        res = sb("res", [CH, 2, NC, ROW])
        wv = sb("wv", [CH, NC, C])
        wa = sb("wa", [CH, NC, 2 * AH])
        ba = sb("ba", [128, AH])
        wp_sb = sb("wp1", [CH, NC, C])
        bp = sb("bp1", [CH, NC])
        gmat = sb("gmat1", [CH, CH])
        xn = sb("xn1", [CH, NC, 2, RAS, SX])
        y = sb("y", [CH, NC, RAS, RAS])
        rowsum = sb("rowsum", [CH, 2, HN, 2 * HALF])
        pooled = sb("pooled", [CH, NC, HALF, 2, IP])
        a = sb("a", [128, HALF, AH])
        top = sb("top1", [128, HC, HALF * KK])
        rtotal = sb("rtotal1", [128, HC, HALF * KK])
        z = sb("z", [CH, PJ * SX])
        t = sb("t", [CH, 2, PJ * IP])
        v = sb("v", [CH, HN, CH])
        o = sb("o1", [CH, HN, PJ])

        consts, zeroed, passed = sem("consts1"), sem("zeroed1"), sem("passed1")
        x_loaded, res_loaded, out_stored = sem("x1_loaded"), sem("res_loaded"), sem("out_stored")
        xn_raw, xn_ready = sem("xn1_raw"), sem("xn1_ready")
        rowsum_ready, pooled_ready = sem("rowsum_ready"), sem("pooled_ready")
        a_raw, a_biased = sem("a_raw"), sem("a_biased")
        top_ready, a_centred, a_exp = sem("top1_ready"), sem("a_centred"), sem("a_exp")
        total_ready, rtotal_ready, a_ready = sem("total1_ready"), sem("rtotal1_ready"), sem("a_ready")
        z_ready, t_ready = sem("z_ready"), sem("t_ready")
        v_raw, v_ready = sem("v1_raw"), sem("v1_ready")
        o_raw, o_ready = sem("o1_raw"), sem("o1_ready")
        folded, y_ready = sem("folded"), sem("y_ready")
        proj_raw, res_done = sem("proj1_raw"), sem("res1_done")
        FOLDS = KK

        stats = Stats(sb, sem, "l1", VB[0:CH, :], gmat, lambda i, row, c: x[:, row, c, :], passed)

        def act_norm(act, i):
            act.wait_ge(stats.step, (i + 1) * STAT_STEPS)
            at(act, v_raw, NG * NB * i)
            for row in range(NWIN):
                for c in range(NC):
                    scale, shift = stats.affine_of(i, c)
                    first = WIN * row + SHIFT + 1
                    for f in range(2):
                        act.activation(xn[:, c, f, first:first + WIN, SHIFT + 1:SX]
                                       .rearrange("p r (w n) -> p w r n", n=WIN),
                                       x[:, row, c, f * ROW // 2:(f + 1) * ROW // 2]
                                       .rearrange("p (w r n) -> p w r n", r=WIN, n=WIN),
                                       ACT.Identity, bias=shift, scale=scale).then_inc(xn_raw, 1)

        def pool_wrap_xn(pool, i):
            pool.wait_ge(xn_raw, 32 * (i + 1))
            pool.sem_inc(passed, 1)
            for c in range(NC):
                pool.tensor_copy(xn[:, c, 0, SHIFT + 1:RAS, 1:SHIFT + 1],
                                 xn[:, c, 1, SHIFT + 1:RAS, SX - SHIFT:SX]).then_inc(xn_ready, 1)
                pool.tensor_copy(xn[:, c, 1, SHIFT + 1:RAS, 0:SHIFT + 1],
                                 xn[:, c, 0, SHIFT + 1:RAS, 2 * HALF:SX]).then_inc(xn_ready, 1)
            pool.wait_ge(xn_ready, 6 * i + 4)
            pool.sem_inc(passed, 1)
            for c in range(NC):
                pool.tensor_copy(xn[:, c, :, 1:SHIFT + 1, :], xn[:, c, :, H + 1:RAS, :]).then_inc(xn_ready, 1)

        def dve_pool(dve, i):
            dve.wait_ge(xn_ready, 6 * (i + 1))
            for c in range(NC):
                at(dve, pooled_ready, 2 * i + c)
                dve.tensor_tensor(rowsum[:, :, :, :], xn[:, c, :, 1:H + 1:2, 1:2 * HALF + 1],
                                  xn[:, c, :, 2:H + 2:2, 1:2 * HALF + 1], ALU.add).then_inc(rowsum_ready, 1)
                dve.wait_ge(rowsum_ready, 2 * i + c + 1)
                pair = rowsum[:, :, :, :].rearrange("p f i (j b) -> p f i j b", b=2)
                dve.tensor_tensor(pooled[:, c, :, :, 0:HN].rearrange("p j f i -> p f i j"),
                                  pair[:, :, :, :, 0], pair[:, :, :, :, 1], ALU.add).then_inc(pooled_ready, 1)

        def pe_logits(pe, i):
            pe.wait_ge(pooled_ready, 2 * (i + 1))
            for jp in range(HALF // 2):
                lb = bank[4 + jp % 2]
                if jp < 2:
                    at(pe, o_ready, NG * NB * i)
                else:
                    pe.wait_ge(a_biased, (HALF // 2) * i + jp - 1)
                for j in range(2):
                    for hc in range(NC):
                        for kc in range(NC):
                            mm = pe.matmul(lb[64 * hc:64 * hc + 64, j * AH:(j + 1) * AH],
                                           pooled[:, kc, 2 * jp + j, :, :].rearrange("p f i -> p (f i)"),
                                           wa[:, kc, hc * AH:(hc + 1) * AH], start=(kc == 0), stop=(kc == NC - 1))
                mm.then_inc(a_raw, 1)

        def part(h):
            return a[:, :, h * KK * KK:(h + 1) * KK * KK].rearrange("P j (p q) -> P j p q", q=KK)

        def dve_logits(dve, i):
            at(dve, z_ready, NH * i)
            for jp in range(HALF // 2):
                dve.wait_ge(a_raw, (HALF // 2) * i + jp + 1)
                dve.scalar_tensor_tensor(out=a[:, 2 * jp:2 * jp + 2, :],
                                         in0=bank[4 + jp % 2][:, 0:2 * AH].rearrange("p (j a) -> p j a", j=2),
                                         scalar=0.25, in1=ba[:, :].unsqueeze(1).broadcast_to([128, 2, AH]),
                                         op0=ALU.mult, op1=ALU.add).then_inc(a_biased, 1)

        def wide(s, h):
            return s[:, h, :].rearrange("P (j p) -> P j p", p=KK).unsqueeze(3).broadcast_to([128, HALF, KK, KK])

        def dve_centre(dve, i, h):
            if h == 0:
                dve.wait_ge(a_biased, (HALF // 2) * (i + 1))
            dve.tensor_reduce(top[:, h, :].rearrange("P (j p) -> P j p", p=KK), part(h), AX.X, ALU.max) \
                .then_inc(top_ready, 1)
            dve.wait_ge(top_ready, HC * i + h + 1)
            dve.tensor_tensor(part(h), part(h), wide(top, h), ALU.subtract).then_inc(a_centred, 1)

        def act_exp(act, i, h):
            act.wait_ge(a_centred, HC * i + h + 1)
            act.activation(part(h), part(h), ACT.Exp, scale=QSCALE).then_inc(a_exp, 1)

        def dve_total(dve, i, h):
            dve.wait_ge(a_exp, HC * i + h + 1)
            at(dve, a_ready, HC * i)
            dve.tensor_reduce(top[:, h, :].rearrange("P (j p) -> P j p", p=KK), part(h), AX.X, ALU.add) \
                .then_inc(total_ready, 1)
            dve.wait_ge(total_ready, HC * i + h + 1)
            dve.reciprocal(rtotal[:, h, :], top[:, h, :]).then_inc(rtotal_ready, 1)

        def dve_softmax(dve, i):
            dve_logits(dve, i)
            dve_centre(dve, i, 0)
            dve_centre(dve, i, 1)
            dve_total(dve, i, 0)
            dve_centre(dve, i, 2)
            dve_total(dve, i, 1)
            dve_total(dve, i, 2)

        def pool_scale(pool, i, h):
            pool.wait_ge(rtotal_ready, HC * i + h + 1)
            pool.tensor_tensor(part(h), part(h), wide(rtotal, h), ALU.mult).then_inc(a_ready, 1)

        def act_spread(act, i, hs):
            g, h = hs // HC, hs % HC
            act.wait_ge(a_ready, HC * i + h + 1)
            at(act, t_ready, NH * i + hs)
            for qy in range(K):
                first = z[32 * qy:32 * qy + 32, 0:1]
                diagonal = bass.AP(first.tensor, first.offset,
                                   [[first.ap[0][0], 32], [HALF * SX, KK], [SX + 2, HALF], [1, K]])
                src = a[32 * g:32 * g + 32, :, h * KK * KK:(h + 1) * KK * KK].rearrange(
                    "P j (p u v) -> P u p j v", u=K, v=K)[:, qy, :, :, :]
                cp = act.activation(diagonal, src, ACT.Copy)
            cp.then_inc(z_ready, 1)

        def dve_turn(dve, i, hs):
            dve.wait_ge(z_ready, NH * i + hs + 1)
            past(dve, o_raw, NB * NH * i + NB * max(hs - 1, 0))
            dve.transpose(t[:, hs % 2, :], z[:, :]).then_inc(t_ready, 1)

        def pe_values(pe, i, g, kb):
            c, f = g // 2, g % 2
            at(pe, v_ready, NB * (NG * i + g) + kb)
            for k in range(IB):
                row = 2 * (IB * kb + k)
                for kc in range(NC):
                    mm = pe.matmul(VB[0:CH, k * CH:(k + 1) * CH],
                                   xn[:, kc, f, row:row + K, :].rearrange("p r x -> p (r x)"),
                                   wv[:, kc, c * CH:(c + 1) * CH], start=(kc == 0), stop=(kc == NC - 1))
            mm.then_inc(v_raw, 1)

        def act_values(act, i, g, kb):
            act.wait_ge(v_raw, NB * (NG * i + g) + kb + 1)
            act.activation(v[:, IB * kb:IB * (kb + 1), :].rearrange("p i d -> p (i d)"),
                           VB[0:CH, 0:IB * CH], ACT.Copy).then_inc(v_ready, 1)

        def pe_head(pe, i, hs, last):
            g, h = hs // HC, hs % HC
            pe.wait_ge(t_ready, NH * i + hs + 1)
            for kb in range(NB):
                if h == 0:
                    pe.wait_ge(v_ready, NB * (NG * i + g) + kb + 1)
                    if g > 0:
                        pe.wait_ge(o_ready, NB * (NG * i + g - 1) + kb + 1)
                for k in range(IB):
                    row = IB * kb + k
                    mm = pe.matmul(bank[kb][32 * h:32 * h + 32, k * PJ:(k + 1) * PJ],
                                   v[:, row, HD * h:HD * (h + 1)],
                                   t[:, hs % 2, :].rearrange("p (n i) -> p n i", i=IP)[:, :, row],
                                   start=True, stop=True)
                mm.then_inc(o_raw, 1)
                if h == HC - 1 and g < NG - 1:
                    pe_values(pe, i, g + 1, kb)

        def act_outputs(act, i, g):
            for kb in range(NB):
                past(act, o_raw, NB * (NH * i + g * HC + HC - 1) + kb + 1)
                past(act, folded, FOLDS * (NG * i + g))
                act.activation(o[:, IB * kb:IB * (kb + 1), :].rearrange("p i n -> p (i n)"),
                               bank[kb][0:CH, 0:IB * PJ], ACT.Copy).then_inc(o_ready, 1)
                if g < NG - 1:
                    act_values(act, i, g + 1, kb)

        def pool_fold(pool, i, g):
            c, f = g // 2, g % 2
            pool.wait_ge(o_ready, NB * (NG * i + g + 1))
            if g == 0:
                past(pool, proj_raw, 2 * NWIN * i)
            pool.sem_inc(passed, 1)
            order = [(1, 1), (1, 2), (2, 1), (2, 2), (0, 1), (0, 2), (1, 0), (2, 0), (0, 0)]
            for n, (py, px) in enumerate(order):
                i0 = 1 if py == 0 else 0
                j0 = 1 if px == 0 and f == 0 else 0
                r0, c0 = 2 * i0 + py, 2 * HALF * f + 2 * j0 + px
                dst = y[:, c, r0:r0 + 2 * (HN - i0) - 1:2, c0:c0 + 2 * (HALF - j0) - 1:2]
                src = o[:, i0:HN, (K * py + px) * HALF + j0:(K * py + px + 1) * HALF]
                if n < 4:
                    pool.tensor_copy(dst, src).then_inc(folded, 1)
                else:
                    past(pool, folded, FOLDS * (NG * i + g) + n)
                    pool.tensor_tensor(dst, dst, src, ALU.add).then_inc(folded, 1)

        def pool_wrap_y(pool, i):
            past(pool, folded, FOLDS * NG * (i + 1))
            pool.sem_inc(passed, 1)
            for c in range(NC):
                pool.tensor_copy(y[:, c, 1:H + 1, W + 1:RAS], y[:, c, 1:H + 1, 1:SHIFT + 1]).then_inc(y_ready, 1)
            pool.wait_ge(y_ready, 4 * i + 2)
            pool.sem_inc(passed, 1)
            for c in range(NC):
                pool.tensor_copy(y[:, c, H + 1:RAS, 1:RAS], y[:, c, 1:SHIFT + 1, 1:RAS]).then_inc(y_ready, 1)

        def pe_proj(pe, i):
            pe.wait_ge(y_ready, 4 * (i + 1))
            for row in range(NWIN):
                n = NWIN * i + row
                if row >= 2:
                    past(pe, res_done, 2 * (n - 1))
                first = WIN * row + SHIFT + 1
                for c in range(NC):
                    for kc in range(NC):
                        mm = pe.matmul(bank[2 * (row % 2) + c][0:CH, 0:ROW], wp_sb[:, kc, c * CH:(c + 1) * CH],
                                       y[:, kc, first:first + WIN, SHIFT + 1:RAS]
                                       .rearrange("p r (w n) -> p w r n", n=WIN),
                                       start=(kc == 0), stop=(kc == NC - 1))
                    mm.then_inc(proj_raw, 1)

        def dve_residual(dve, i):
            for row in range(NWIN):
                n = NWIN * i + row
                dve.wait_ge(res_loaded, 16 * (n + 1))
                for c in range(NC):
                    past(dve, proj_raw, 2 * n + c + 1)
                    r = res[:, row % 2, c, :]
                    dve.scalar_tensor_tensor(out=r, in0=bank[2 * (row % 2) + c][0:CH, 0:ROW],
                                             scalar=bp[:, c:c + 1], in1=r, op0=ALU.add, op1=ALU.add) \
                        .then_inc(res_done, 1)

        block = ctx.enter_context(nc.Block())

        @block.sync
        def _(sp):
            for src, dst in ((w_v, wv[:, :, :]), (w_a, wa[:, :, :]), (w_proj, wp_sb[:, :, :]),
                             (b_proj, bp[:, :]), (gmat_d, gmat[:, :]),
                             (b_a[0:1, :].broadcast_to([64, AH]), ba[0:64, :]),
                             (b_a[1:2, :].broadcast_to([64, AH]), ba[64:128, :])):
                sp.dma_start(dst, src).then_inc(consts, 16)

            def load_image(i):
                sp.dma_start(x[:, :, :, :].rearrange("p a c n -> p (a c n)"),
                             x1[bass.ds(i, 1), :, :].rearrange("a p n -> (a p) n")).then_inc(x_loaded, 16)

            def load_row(n, i, row):
                sp.dma_start(res[:, row % 2, :, :].rearrange("p c n -> p (c n)"),
                             x1[bass.ds(i, 1), :, NC * ROW * row:NC * ROW * (row + 1)]
                             .rearrange("a p n -> (a p) n")).then_inc(res_loaded, 16)

            def rows(i, last):
                for row in range(NWIN):
                    n = NWIN * i + row
                    past(sp, res_done, 2 * (n + 1))
                    sp.dma_start(out[bass.ds(i, 1), :, NC * ROW * row:NC * ROW * (row + 1)]
                                 .rearrange("a p n -> (a p) n"),
                                 res[:, row % 2, :, :].rearrange("p c n -> p (c n)")).then_inc(out_stored, 16)
                    sp.wait_ge(out_stored, 16 * (n + 1))
                    if not (last and row >= NWIN - 2):
                        sp.wait_ge(res_loaded, 16 * (n + 2))
                        nxt = row + 2
                        load_row(n + 2, i + nxt // NWIN, nxt % NWIN)

            load_image(0)
            load_row(0, 0, 0)
            sp.wait_ge(res_loaded, 16)
            load_row(1, 0, 1)
            with sp.Fori(0, B - 1) as i:
                sp.wait_ge(xn_raw, 32 * (i + 1))
                load_image(i + 1)
                rows(i, False)
            rows(B - 1, True)

        @block.gpsimd
        def _(pool):
            start_at_one(pool, o_raw, folded, proj_raw, res_done)
            for t0 in (xn[:, :, :, :, :], pooled[:, :, :, :, :], z[:, :], y[:, :, :, :]):
                pool.memset(t0, 0.0).then_inc(zeroed, 1)
            pool_wrap_xn(pool, 0)
            for h in range(HC):
                pool_scale(pool, 0, h)

            def image(i, last):
                for g in range(NG - 1):
                    pool_fold(pool, i, g)
                if not last:
                    pool_wrap_xn(pool, i + 1)
                pool_fold(pool, i, NG - 1)
                pool_wrap_y(pool, i)
                if not last:
                    for h in range(HC):
                        pool_scale(pool, i + 1, h)

            with pool.Fori(0, B - 1) as i:
                image(i, False)
            image(B - 1, True)

        @block.vector
        def _(dve):
            dve.wait_ge(consts, 16 * 7)
            dve.wait_ge(zeroed, 4)
            dve.wait_ge(x_loaded, 16)
            stats.rows(dve, 0, range(NWIN))
            stats.aggregate(dve, 0)
            stats.spread(dve, 0)
            stats.variance(dve, 0)
            stats.affine(dve, 0)
            dve_pool(dve, 0)
            dve_softmax(dve, 0)

            def image(i, last):
                for hs in range(NH):
                    dve_turn(dve, i, hs)
                    if last:
                        continue
                    if hs == 0:
                        dve.wait_ge(x_loaded, 16 * (i + 2))
                    if hs < 4:
                        stats.rows(dve, i + 1, (2 * hs, 2 * hs + 1))
                    if hs == 3:
                        stats.aggregate(dve, i + 1)
                    if hs == 5:
                        stats.spread(dve, i + 1)
                    if hs == 7:
                        stats.variance(dve, i + 1)
                    if hs == 8:
                        stats.affine(dve, i + 1)
                if not last:
                    dve_pool(dve, i + 1)
                    dve_softmax(dve, i + 1)
                dve_residual(dve, i)

            with dve.Fori(0, B - 1) as i:
                image(i, False)
            image(B - 1, True)

        @block.scalar
        def _(act):
            act.wait_ge(zeroed, 4)
            act.wait_ge(x_loaded, 16)

            def begin(i):
                for h in range(HC):
                    act_exp(act, i, h)
                act_spread(act, i, 0)
                for kb in range(NB):
                    act_values(act, i, 0, kb)

            stats.root(act, 0)
            act_norm(act, 0)
            begin(0)

            def image(i, last):
                for hs in range(NH):
                    if hs + 1 < NH:
                        act_spread(act, i, hs + 1)
                    if hs == 7 and not last:
                        stats.root(act, i + 1)
                    if hs == NH - HC and not last:
                        act.wait_ge(x_loaded, 16 * (i + 2))
                        act_norm(act, i + 1)
                    if hs % HC == HC - 1:
                        act_outputs(act, i, hs // HC)
                if not last:
                    begin(i + 1)

            with act.Fori(0, B - 1) as i:
                image(i, False)
            image(B - 1, True)

        @block.tensor
        def _(pe):
            pe.wait_ge(consts, 16 * 7)
            pe.wait_ge(zeroed, 4)
            stats.mean_mm(pe, 0)
            stats.var_mm(pe, 0)
            pe_logits(pe, 0)
            pe.wait_ge(stats.step, STAT_STEPS)
            for kb in range(NB):
                pe_values(pe, 0, 0, kb)

            def image(i, last):
                pe.wait_ge(a_biased, (HALF // 2) * (i + 1))
                past(pe, res_done, 2 * NWIN * i)
                for hs in range(NH):
                    if hs in (5, 8) and not last:
                        pe.wait_ge(stats.step, (i + 1) * STAT_STEPS + (20 if hs == 5 else 23))
                    pe_head(pe, i, hs, last)
                    if hs == 4 and not last:
                        pe.wait_ge(v_ready, NB * (NG * i + 2))
                        stats.mean_mm(pe, i + 1)
                    if hs == 6 and not last:
                        pe.wait_ge(v_ready, NB * (NG * i + 3))
                        stats.var_mm(pe, i + 1)
                if not last:
                    pe_logits(pe, i + 1)
                pe_proj(pe, i)
                if not last:
                    for kb in range(NB):
                        pe_values(pe, i + 1, 0, kb)

            with pe.Fori(0, B - 1) as i:
                image(i, False)
            image(B - 1, True)


def preact_block(nc, x, w_qkv, b_qk, b_v, w_proj, b_proj, rel, mask, gmat, kmask, ident, w_v, w_a, b_a,
                 w_proj1, b_proj1, out):
    x1 = nc.dram_tensor("x1_scratch", [B, CH, NWIN * NC * ROW], F32, kind="Internal").ap()
    window_layer(nc, x, x1, w_qkv, b_qk, b_v, w_proj, b_proj, rel, mask, gmat, kmask, ident)
    outlook_layer(nc, x1, out, w_v, w_a, b_a, w_proj1, b_proj1, gmat)



def shift_mask():
    region = np.zeros((H, W), np.float32)
    cuts = ((0, H - WIN), (H - WIN, H - SHIFT), (H - SHIFT, H))
    for n, (h0, h1) in enumerate(cuts):
        for m, (w0, w1) in enumerate(cuts):
            region[h0:h1, w0:w1] = 3 * n + m
    win = region.reshape(NWIN, WIN, NWIN, WIN).transpose(0, 2, 1, 3).reshape(NWIN, NWIN, NTOK)
    out = np.zeros((2, PADW, 2, PAIRS, NTOK), np.float32)
    for last_row, wy in enumerate((0, NWIN - 1)):
        for wx in range(NWIN):
            differ = win[wy, wx][:, None] != win[wy, wx][None, :]
            out[wx % 2, :NTOK, last_row, wx // 2] = np.where(differ, np.float32(-100), np.float32(0))
    return out.reshape(128, 2, PAIRS, NTOK)


def rel_index():
    coords = np.stack(np.meshgrid(np.arange(WIN), np.arange(WIN), indexing="ij")).reshape(2, -1)
    rel = coords[:, :, None] - coords[:, None, :] + WIN - 1
    return rel[0] * (2 * WIN - 1) + rel[1]



def to_windows(x):
    x = np.roll(x, (-SHIFT, -SHIFT), axis=(1, 2))
    x = x.reshape(B, NWIN, WIN, NWIN, WIN, NC, CH).transpose(0, 6, 1, 5, 3, 2, 4)
    return np.ascontiguousarray(x.reshape(B, CH, NWIN * NC * ROW))


def from_windows(x):
    x = x.reshape(B, CH, NWIN, NC, NWIN, WIN, WIN).transpose(0, 2, 5, 4, 6, 3, 1)
    return np.ascontiguousarray(np.roll(x.reshape(B, H, W, C), (SHIFT, SHIFT), axis=(1, 2)))


def kernel(**inputs):
    import concourse.bacc as _bacc
    from concourse.bass_utils import run_bass_kernel_spmd as _run

    a = {k: np.asarray(v) for k, v in inputs.items()}

    def chunked(w):
        return np.ascontiguousarray(w.reshape(NC, CH, -1).transpose(1, 0, 2))

    qkv_b = a["L0_conv_qkv_bias"]
    b_v = np.zeros((128, 2), np.float32)
    b_v[:, 0] = qkv_b[2 * C:2 * C + 128]
    b_v[0:64, 1] = qkv_b[2 * C + 128:]
    rel = np.zeros((2, PADW, HEADS, NTOK), np.float32)
    rel[:, :NTOK] = a["L0_conv_rel_bias_table"][rel_index()].transpose(0, 2, 1)[None]
    arrays = {
        "x": to_windows(a["x"]),
        "w_qkv": chunked(a["L0_conv_qkv_weight"].T),
        "b_qk": np.ascontiguousarray(qkv_b[:2 * C].reshape(4, CH).T),
        "b_v": b_v,
        "w_proj": np.ascontiguousarray(a["L0_conv_proj_weight"].T),
        "b_proj": np.ascontiguousarray(a["L0_conv_proj_bias"].reshape(NC, CH).T),
        "rel": rel.reshape(128, HEADS, NTOK),
        "mask": shift_mask(),
        "gmat": np.kron(np.eye(CH // GC), np.full((GC, GC), 1.0 / GC)).astype(np.float32),
        "kmask": np.kron(np.eye(HC), np.ones((HD, 1))).astype(np.float32),
        "ident": np.eye(128, dtype=np.float32),
        "w_v": chunked(a["L1_conv_Wv"]),
        "w_a": chunked(a["L1_conv_Wa"]),
        "b_a": np.ascontiguousarray(a["L1_conv_ba"].reshape(NC, AH)),
        "w_proj1": chunked(a["L1_conv_Wp"]),
        "b_proj1": np.ascontiguousarray(a["L1_conv_bp"].reshape(NC, CH).T),
    }
    nc = _bacc.Bacc("TRN2", target_bir_lowering=False, num_devices=1)
    aps = [nc.dram_tensor("in_" + name, v.shape, F32, kind="ExternalInput").ap() for name, v in arrays.items()]
    out = nc.dram_tensor("out", [B, CH, NWIN * NC * ROW], F32, kind="ExternalOutput").ap()
    preact_block(nc, *aps, out)
    r = _run(nc, [{"in_" + k: v for k, v in arrays.items()}], core_ids=[0])
    return from_windows(r.results[0]["out"])
```

```python
from contextlib import ExitStack

import numpy as np
import concourse.bass as bass
from concourse import mybir

F32 = mybir.dt.float32
ALU = mybir.AluOpType
ACT = mybir.ActivationFunctionType
AX = mybir.AxisListType

B, H, W, C = 32, 56, 56, 192
HEADS, HD = 6, 32
WIN, SHIFT = 7, 3
NTOK = WIN * WIN
NWIN = H // WIN
ROW = NWIN * NTOK
CH = 96
NC = C // CH
HC = HEADS // NC
GROUPS = 32
GC = C // GROUPS
GN_EPS = 1e-5
PADW = 64
PAIRS = NWIN // 2
QSCALE = HD ** -0.5
LOGIT = HC * NTOK
K = 3
KK = K * K
HN = H // 2
HALF = HN // 2
SX = 32
IP = 32
RAS = 60
XT = 2 * HALF + 1
TC = K * XT
AH = HC * KK * KK
BN = 6
STAT_STEPS = 16 + 2 + 4 + 3


def at(eng, sem, value):
    if isinstance(value, int) and value <= 0:
        return
    eng.wait_ge(sem, value)




def past(eng, sem, value):
    at(eng, sem, value + 1)


def start_at_one(eng, *sems):
    for s in sems:
        eng.sem_inc(s, 1)


class Stats:

    def __init__(self, sb, sem, tag, psum, gmat, x_row, passed):
        self.bn = sb("bn_" + tag, [CH, NC, NWIN, BN])
        self.mv = sb("mv_" + tag, [CH, NC, 2])
        self.dev = sb("dev_" + tag, [CH, NC])
        self.gmean = sb("gmean_" + tag, [CH, NC])
        self.norm = sb("norm_" + tag, [CH, 2, 2, NC])
        self.var = sb("var_" + tag, [CH, NC])
        self.std = sb("std_" + tag, [CH, NC])
        self.rooted = sem("rooted_" + tag)
        self.passed = passed
        self.step = sem("stat_step_" + tag)
        self.mm = sem("stat_mm_" + tag)
        self.psum, self.gmat, self.x_row = psum, gmat, x_row

    def rows(self, dve, i, rows):
        for row in rows:
            for c in range(NC):
                out = self.bn[:, c, bass.ds(row, 1), :].rearrange("p a n -> p (a n)")
                dve.bn_stats(out, self.x_row(i, row, c)).then_inc(self.step, 1)

    def aggregate(self, dve, i):
        dve.wait_ge(self.step, i * STAT_STEPS + 16)
        dve.sem_inc(self.passed, 1)
        for c in range(NC):
            dve.bn_aggr(self.mv[:, c, :], self.bn[:, c, :, :].rearrange("p a b -> p (a b)")) \
                .then_inc(self.step, 1)

    def mean_mm(self, pe, i):
        pe.wait_ge(self.step, i * STAT_STEPS + 18)
        pe.matmul(self.psum[:, 0:NC], self.gmat[:, :], self.mv[:, :, 0], start=True, stop=True) \
            .then_inc(self.mm, 1)

    def spread(self, dve, i):
        dve.wait_ge(self.mm, 2 * i + 1)
        dve.tensor_tensor(self.dev[:, :], self.mv[:, :, 0], self.psum[:, 0:NC], ALU.subtract) \
            .then_inc(self.step, 1)
        dve.tensor_copy(self.gmean[:, :], self.psum[:, 0:NC]).then_inc(self.step, 1)
        dve.wait_ge(self.step, i * STAT_STEPS + 20)
        dve.tensor_tensor(self.dev[:, :], self.dev[:, :], self.dev[:, :], ALU.mult) \
            .then_inc(self.step, 1)
        dve.wait_ge(self.step, i * STAT_STEPS + 21)
        dve.tensor_tensor(self.dev[:, :], self.dev[:, :], self.mv[:, :, 1], ALU.add) \
            .then_inc(self.step, 1)

    def var_mm(self, pe, i):
        pe.wait_ge(self.step, i * STAT_STEPS + 22)
        pe.matmul(self.psum[:, 0:NC], self.gmat[:, :], self.dev[:, :], start=True, stop=True) \
            .then_inc(self.mm, 1)

    def variance(self, dve, i):
        dve.wait_ge(self.mm, 2 * i + 2)
        dve.tensor_scalar(self.var[:, :], self.psum[:, 0:NC], GN_EPS, None, ALU.add).then_inc(self.step, 1)

    def root(self, act, i):
        act.wait_ge(self.step, i * STAT_STEPS + 23)
        act.activation(self.std[:, :], self.var[:, :], ACT.Sqrt).then_inc(self.rooted, 1)

    def affine(self, dve, i):
        scale = self.norm[:, bass.ds(i % 2, 1), 0, :].rearrange("p a c -> p (a c)")
        bias = self.norm[:, bass.ds(i % 2, 1), 1, :].rearrange("p a c -> p (a c)")
        dve.wait_ge(self.rooted, i + 1)
        dve.reciprocal(scale, self.std[:, :]).then_inc(self.step, 1)
        dve.wait_ge(self.step, i * STAT_STEPS + 24)
        dve.scalar_tensor_tensor(out=bias, in0=self.gmean[:, :], scalar=-1.0, in1=scale,
                                 op0=ALU.mult, op1=ALU.mult).then_inc(self.step, 1)

    def affine_of(self, i, c):
        return (self.norm[:, bass.ds(i % 2, 1), 0, c], self.norm[:, bass.ds(i % 2, 1), 1, c])


def window_layer(nc, x_in, x1, mv1, w_qkv, b_qk, b_v, w_proj, b_proj, rel, mask, gmat_d, kmask_d, ident_d):
    with ExitStack() as ctx:
        def sb(name, shape):
            return ctx.enter_context(nc.sbuf_tensor(name, shape, F32))

        def sem(name):
            return ctx.enter_context(nc.semaphore(name))

        bank = [ctx.enter_context(nc.psum_tensor(f"l0_bank{i}", [128, 512], F32)) for i in range(8)]
        QK, VB, PT, OB = bank[0:2], bank[2], bank[5:7], bank[7]
        SB = bank[3:5]

        x = sb("x", [CH, 2 * NWIN, NC, ROW])
        wqkv = sb("wqkv", [CH, NC, 3 * C])
        wp_sb = sb("wp_sb", [128, 2, C])
        bqk = sb("bqk", [CH, 4])
        bqs = sb("bqs", [CH, NC])
        bkm = sb("bkm", [CH, HC])
        bv = sb("bv", [128, 2])
        bp = sb("bp", [CH, NC])
        gmat = sb("gmat", [CH, CH])
        kmask = sb("kmask", [CH, HC])
        ident = sb("ident", [128, 128])
        rel_sb = sb("rel_sb", [128, HEADS, NTOK])
        mask_sb = sb("mask_sb", [128, 2, PAIRS, NTOK])
        bias = sb("bias", [128, 2, PAIRS, HEADS, NTOK])
        xn = sb("xn", [CH, 2, NC, NWIN, PADW])
        q = sb("q", [CH, 2, NC, NWIN, PADW])
        kbd = sb("kbd", [CH, 2, NC, HC, ROW])
        vbd = sb("vbd", [128, 2, NWIN, 3, 2 * HD])
        logit = sb("logit", [128, PAIRS, HEADS, NTOK])
        prob = sb("prob", [128, 2, PAIRS, HEADS, PADW])
        top = sb("top", [128, PAIRS * HEADS])
        total = sb("total", [128, PAIRS * HEADS])
        rtotal = sb("rtotal", [128, PAIRS * HEADS])
        pt = sb("pt", [128, 2, 3, 128])
        o = sb("o", [128, 2, 2, ROW])
        aggregate = sb("aggregate", [CH, NC, 2])
        bn1 = sb("bn1", [CH, NC, NWIN, BN])

        consts = sem("consts")
        zeroed = sem("zeroed")
        bias_ready = sem("bias_ready")
        x_loaded = sem("x_loaded")
        x_stored = sem("x_stored")
        xn_ready = sem("xn_ready")
        q_raw, q_ready = sem("q_raw"), sem("q_ready")
        k_raw, k_first, k_second = sem("k_raw"), sem("k_first"), sem("k_second")
        v_raw, v_ready = sem("v_raw"), [sem("v_first"), sem("v_second")]
        s_raw, s_biased = sem("s_raw"), sem("s_biased")
        top_ready, centred = sem("top_ready"), sem("centred")
        exp_ready, total_ready, rtotal_ready = sem("exp_ready"), sem("total_ready"), sem("rtotal_ready")
        prob_ready = sem("prob_ready")
        pt_raw, pt_ready = sem("pt_raw"), sem("pt_ready")
        pv_done = sem("pv_done")
        o_raw, o_ready = sem("o_raw"), sem("o_ready")
        proj_raw, res_done = sem("proj_raw"), [sem("res_first"), sem("res_second")]
        measured, summed_up = sem("measured"), sem("summed_up")

        NCONST = 11
        stats = Stats(sb, sem, "l0", OB[0:CH, :], gmat,
                      lambda i, row, c: x[:, bass.ds((i * NWIN + row) % (2 * NWIN), 1), c, :]
                      .rearrange("p a n -> p (a n)"), sem("passed"))

        def x_row(r, c):
            return x[:, bass.ds(r % (2 * NWIN), 1), c, :].rearrange("p a (w n) -> p (a w) n", n=NTOK)


        def act_norm(act, r, i, s):
            at(act, stats.step, (i + 1) * STAT_STEPS)
            at(act, v_raw, 2 * (r - 1))
            for c in range(NC):
                scale, shift = stats.affine_of(i, c)
                act.activation(xn[:, s, c, :, 0:NTOK], x_row(r, c), ACT.Identity, bias=shift,
                               scale=scale).then_inc(xn_ready, 1)

        def pe_qk(pe, r, s, which):
            pe.wait_ge(xn_ready, 2 * (r + 1))
            for c in range(NC):
                if which == 0:
                    past(pe, res_done[c], r - 1)
                else:
                    pe.wait_ge(q_ready, 2 * r + c + 1)
                for kc in range(NC):
                    mm = pe.matmul(QK[c][0:CH, 0:ROW], wqkv[:, kc, which * C + c * CH:which * C + (c + 1) * CH],
                                   xn[:, s, kc, :, 0:NTOK], start=(kc == 0), stop=(kc == NC - 1))
                mm.then_inc(k_raw if which else q_raw, 1)

        def act_q(act, r, s):
            past(act, s_raw, 2 * (r - 1))
            for c in range(NC):
                act.wait_ge(q_raw, 2 * r + c + 1)
                act.activation(q[:, s, c, :, 0:NTOK],
                               QK[c][0:CH, 0:ROW].rearrange("p (w n) -> p w n", n=NTOK), ACT.Identity,
                               bias=bqs[:, c:c + 1], scale=QSCALE).then_inc(q_ready, 1)


        def dve_k(dve, r, s):
            past(dve, s_raw, 2 * (r - 1))
            dve.wait_ge(k_raw, 2 * r + 1)
            dve.scalar_tensor_tensor(
                out=kbd[:, s, 0, :, :],
                in0=QK[0][0:CH, 0:ROW].unsqueeze(1).broadcast_to([CH, HC, ROW]),
                scalar=bqk[:, NC:NC + 1],
                in1=kmask[:, :].unsqueeze(2).broadcast_to([CH, HC, ROW]),
                op0=ALU.add, op1=ALU.mult).then_inc(k_first, 1)

        def act_k(act, r, s):
            past(act, s_raw, 2 * (r - 1))
            act.wait_ge(k_raw, 2 * r + 2)
            for h in range(HC):
                act.activation(kbd[:, s, 1, h, :], QK[1][0:CH, 0:ROW], ACT.Identity,
                               bias=bkm[:, h:h + 1], scale=kmask[:, h:h + 1]).then_inc(k_second, 1)

        def pe_v(pe, r, s, half):
            at(pe, v_ready[1 - half], 4 * (r + half))
            for p in range(2):
                for kc in range(NC):
                    mm = pe.matmul(VB[:, p * C:(p + 1) * C],
                                   xn[:, s, kc, 4 * half + 2 * p:4 * half + 2 * p + 2, :]
                                   .rearrange("p w n -> p (w n)"),
                                   wqkv[:, kc, 2 * C:3 * C], start=(kc == 0), stop=(kc == NC - 1))
            mm.then_inc(v_raw, 1)


        def v_pieces(s, half):
            return [(vbd[64 * odd:64 * odd + 64, s, 4 * half + w:4 * half + w + 3:2, :, odd * HD:(odd + 1) * HD],
                     VB[64 * w:64 * w + 64, 0:2 * C].rearrange("p (a h o d) -> p a h o d", a=2, h=3, o=2)
                     [:, :, :, odd, :]) for w in range(2) for odd in range(2)]

        def dve_v(dve, r, s):
            past(dve, pv_done, 4 * (r - 1))
            dve.wait_ge(v_raw, 2 * r + 1)
            for dst, values in v_pieces(s, 0):
                dve.tensor_copy(dst, values).then_inc(v_ready[0], 1)

        def act_v(act, r, s):
            past(act, pv_done, 4 * (r - 1))
            act.wait_ge(v_raw, 2 * r + 2)
            for dst, values in v_pieces(s, 1):
                act.activation(dst, values, ACT.Copy).then_inc(v_ready[1], 1)

        def pe_logits(pe, r, s, half):
            pe.wait_ge(k_first, r + 1)
            pe.wait_ge(k_second, HC * (r + 1))
            at(pe, s_biased, 2 * r + half)
            for p in range(2):
                for w in range(2):
                    win = 4 * half + 2 * p + w
                    for c in range(NC):
                        mm = pe.matmul(SB[p][64 * w:64 * w + 64, c * LOGIT:(c + 1) * LOGIT],
                                       q[:, s, c, win, :],
                                       kbd[:, s, c, :, win * NTOK:(win + 1) * NTOK],
                                       start=True, stop=True)
            mm.then_inc(s_raw, 1)

        def dve_bias(dve, r, half, last_row):
            past(dve, s_raw, 2 * r + half + 1)
            at(dve, exp_ready, r)
            for p in range(2):
                add = dve.tensor_tensor(
                    logit[:, 2 * half + p, :, :].rearrange("p h m -> p (h m)"),
                    SB[p][:, 0:2 * LOGIT],
                    bias[:, last_row, 2 * half + p, :, :].rearrange("p h m -> p (h m)"), ALU.add)
            add.then_inc(s_biased, 1)

        def half_of(s4, half):
            return s4[:, 2 * half:2 * half + 2, :, 0:NTOK].rearrange("p a h m -> p (a h) m")

        def dve_centre(dve, r, half):
            first, n = half * 2 * HEADS, 2 * HEADS
            dve.wait_ge(s_biased, 2 * r + half + 1)
            dve.tensor_reduce(top[:, first:first + n], half_of(logit, half), AX.X, ALU.max) \
                .then_inc(top_ready, 1)
            dve.wait_ge(top_ready, 2 * r + half + 1)
            dve.tensor_tensor(half_of(logit, half), half_of(logit, half),
                              top[:, first:first + n].unsqueeze(2).broadcast_to([128, n, NTOK]),
                              ALU.subtract).then_inc(centred, 1)

        def act_exp(act, r, s):
            act.wait_ge(centred, 2 * (r + 1))
            past(act, pt_raw, 4 * (r - 1))
            act.activation(prob[:, s, :, :, 0:NTOK].rearrange("p a h m -> p (a h) m"),
                           logit[:, :, :, :].rearrange("p a h m -> p (a h) m"), ACT.Exp) \
                .then_inc(exp_ready, 1)

        def dve_total(dve, r, s):
            dve.wait_ge(exp_ready, r + 1)
            at(dve, prob_ready, r)
            dve.tensor_reduce(total[:, :], prob[:, s, :, :, 0:NTOK].rearrange("p a h m -> p (a h) m"),
                              AX.X, ALU.add).then_inc(total_ready, 1)
            dve.wait_ge(total_ready, r + 1)
            dve.reciprocal(rtotal[:, :], total[:, :]).then_inc(rtotal_ready, 1)

        def pool_scale(pool, r, s):
            pool.wait_ge(rtotal_ready, r + 1)
            pr = prob[:, s, :, :, 0:NTOK].rearrange("p a h m -> p (a h) m")
            pool.tensor_tensor(pr, pr, rtotal[:, :].unsqueeze(2).broadcast_to([128, PAIRS * HEADS, NTOK]),
                               ALU.mult).then_inc(prob_ready, 1)

        def pe_turn(pe, r, s, p):
            if p == 0:
                pe.wait_ge(prob_ready, r + 1)
            past(pe, pt_ready, 4 * r + max(p - 1, 0))
            for hp in range(3):
                mm = pe.transpose(PT[p % 2][:, hp * 128:(hp + 1) * 128],
                                  prob[:, s, p, 2 * hp:2 * hp + 2, :].rearrange("p h m -> p (h m)"),
                                  ident[:, :])
            mm.then_inc(pt_raw, 1)

        def pe_attend(pe, r, s, p):
            past(pe, pt_ready, 4 * r + p + 1)
            if p == 0:
                for half in range(2):
                    pe.wait_ge(v_ready[half], 4 * (r + 1))
            if p % 2 == 0:
                past(pe, o_ready, 2 * r + p // 2)
            for w in range(2):
                col = (2 * (p % 2) + w) * NTOK
                for hp in range(3):
                    rows = 64 * (hp % 2)
                    cols = col + (hp // 2) * (ROW // 2)
                    mm = pe.matmul(OB[rows:rows + 64, cols:cols + NTOK], vbd[:, s, 2 * p + w, hp, :],
                                   pt[:, p % 2, hp, 64 * w:64 * w + NTOK], start=True, stop=True)
            mm.then_inc(pv_done, 1)

        def act_turned(act, r, p):
            past(act, pt_raw, 4 * r + p + 1)
            past(act, pv_done, 4 * r + max(p - 1, 0))
            act.activation(pt[:, p % 2, :, :].rearrange("p h n -> p (h n)"), PT[p % 2][:, 0:384],
                           ACT.Copy).then_inc(pt_ready, 1)

        def act_outputs(act, r, s, half):
            past(act, pv_done, 4 * r + 2 * half + 2)
            lo, hi = half * (ROW // 2), (half + 1) * (ROW // 2)
            act.activation(o[:, s, 0, lo:hi], OB[:, 0:ROW // 2], ACT.Identity, bias=bv[:, 0:1])
            act.activation(o[0:64, s, 1, lo:hi], OB[0:64, ROW // 2:ROW], ACT.Identity,
                           bias=bv[0:64, 1:2]).then_inc(o_ready, 1)

        def pe_proj(pe, r, s, k_after):
            past(pe, o_ready, 2 * (r + 1))
            for c in range(NC):
                if k_after and c == 0:
                    pe.wait_ge(k_first, r + 2)
                elif k_after:
                    pe.wait_ge(k_second, HC * (r + 2))
                else:
                    past(pe, res_done[c], r)
                pe.matmul(QK[c][0:CH, 0:ROW], wp_sb[:, 0, c * CH:(c + 1) * CH], o[:, s, 0, :],
                          start=True, stop=False)
                pe.matmul(QK[c][0:CH, 0:ROW], wp_sb[0:64, 1, c * CH:(c + 1) * CH], o[0:64, s, 1, :],
                          start=False, stop=True).then_inc(proj_raw, 1)

        def dve_residual(dve, r):
            for c in range(NC):
                dve.wait_ge(proj_raw, 2 * r + c + 1)
                row = x[:, bass.ds(r % (2 * NWIN), 1), c, :].rearrange("p a n -> p (a n)")
                dve.scalar_tensor_tensor(out=row, in0=QK[c][0:CH, 0:ROW], scalar=bp[:, c:c + 1], in1=row,
                                         op0=ALU.add, op1=ALU.add).then_inc(res_done[c], 1)

        def dve_measure(dve, r, i, row):
            for c in range(NC):
                past(dve, res_done[c], r + 1)
            past(dve, summed_up, 3 * i)
            dve.sem_inc(stats.passed, 1)
            for c in range(NC):
                dve.bn_stats(bn1[:, c, bass.ds(row, 1), :].rearrange("p a n -> p (a n)"),
                             x[:, bass.ds(r % (2 * NWIN), 1), c, :].rearrange("p a n -> p (a n)")) \
                    .then_inc(measured, 1)

        def dve_sum_up(dve, i):
            dve.wait_ge(measured, 2 * NWIN * (i + 1))
            dve.sem_inc(stats.passed, 1)
            for c in range(NC):
                dve.bn_aggr(aggregate[:, c, :], bn1[:, c, :, :].rearrange("p a b -> p (a b)"))                     .then_inc(summed_up, 1)
            past(dve, summed_up, 3 * i + 2)
            dve.tensor_copy(mv1[:, bass.ds(i, 1), :, :].rearrange("p a c n -> p (a c n)"),
                            aggregate[:, :, :].rearrange("p c n -> p (c n)")).then_inc(summed_up, 1)


        def pe_step(pe, r, s, attend=True, front=True, statistics=None):
            if front:
                pe_qk(pe, r + 1, 1 - s, 0)
                pe_qk(pe, r + 1, 1 - s, 1)
            if statistics is not None:
                stats.mean_mm(pe, statistics)
            if front:
                pe_v(pe, r + 1, 1 - s, 0)
            if attend:
                pe_turn(pe, r, s, 0)
                pe_turn(pe, r, s, 1)
            if front:
                pe_logits(pe, r + 1, 1 - s, 0)
            if attend:
                if statistics is not None:
                    stats.var_mm(pe, statistics)
                    pe.wait_ge(stats.step, statistics * STAT_STEPS + 23)
                pe_attend(pe, r, s, 0)
                pe_turn(pe, r, s, 2)
                pe_attend(pe, r, s, 1)
                pe_turn(pe, r, s, 3)
            if front:
                pe_logits(pe, r + 1, 1 - s, 1)
            if attend:
                pe_attend(pe, r, s, 2)
                pe_attend(pe, r, s, 3)
            if front:
                pe_v(pe, r + 1, 1 - s, 1)
            if attend:
                pe_proj(pe, r, s, front)

        def dve_step(dve, r, s, attend=True, front=True, last_row=0, statistics=None):
            if front:
                dve_k(dve, r + 1, 1 - s)
                if statistics is not None:
                    stats.spread(dve, statistics)
                dve_v(dve, r + 1, 1 - s)
                if statistics is not None:
                    stats.variance(dve, statistics)
                for half in range(2):
                    dve_bias(dve, r + 1, half, last_row)
                    dve_centre(dve, r + 1, half)
            if statistics is not None:
                stats.affine(dve, statistics)
            if attend:
                dve_residual(dve, r)
            if front:
                dve_total(dve, r + 1, 1 - s)

        def act_step(act, r, s, attend=True, front=True, image=None, statistics=None):
            if front:
                act_q(act, r + 1, 1 - s)
                act_k(act, r + 1, 1 - s)
            if attend:
                act_turned(act, r, 0)
                act_turned(act, r, 1)
                act_turned(act, r, 2)
                act_outputs(act, r, s, 0)
                act_turned(act, r, 3)
                act_outputs(act, r, s, 1)
            if statistics is not None:
                stats.root(act, statistics)
            if image is not None:
                act_norm(act, r + 2, image, s)
            if front:
                act_v(act, r + 1, 1 - s)
                act_exp(act, r + 1, 1 - s)

        block = ctx.enter_context(nc.Block())

        @block.sync
        def _(sp):
            for src, dst in ((w_qkv, wqkv[:, :, :]), (w_proj[0:128, :], wp_sb[:, 0, :]),
                             (w_proj[128:192, :], wp_sb[0:64, 1, :]), (b_qk, bqk[:, :]), (b_v, bv[:, :]),
                             (b_proj, bp[:, :]), (gmat_d, gmat[:, :]), (kmask_d, kmask[:, :]),
                             (ident_d, ident[:, :]), (rel, rel_sb[:, :, :]), (mask, mask_sb[:, :, :, :])):
                sp.dma_start(dst, src).then_inc(consts, 16)

            def load(i, slot):
                sp.dma_start(x[:, slot * NWIN:(slot + 1) * NWIN, :, :].rearrange("p a c n -> p (a c n)"),
                             x_in[bass.ds(i, 1), :, :].rearrange("a p n -> (a p) n")).then_inc(x_loaded, 16)

            def store(i, slot):
                for c in range(NC):
                    past(sp, res_done[c], NWIN * (i + 1))
                sp.dma_start(x1[bass.ds(i, 1), :, :].rearrange("a p n -> (a p) n"),
                             x[:, slot * NWIN:(slot + 1) * NWIN, :, :].rearrange("p a c n -> p (a c n)")) \
                    .then_inc(x_stored, 16)
                sp.wait_ge(x_stored, 16 * (i + 1))

            load(0, 0)
            sp.wait_ge(x_loaded, 16)
            load(1, 1)
            with sp.Fori(0, B // 2 - 1) as pair:
                for slot in range(2):
                    store(2 * pair + slot, slot)
                    sp.wait_ge(x_loaded, 16 * (2 * pair + slot + 2))
                    sp.wait_ge(measured, 2 * NWIN * (2 * pair + slot + 1))
                    load(2 * pair + slot + 2, slot)
            for slot in range(2):
                store(B - 2 + slot, slot)

        @block.gpsimd
        def _(pool):
            start_at_one(pool, *res_done, summed_up, s_raw, pv_done, pt_raw, pt_ready, o_ready)
            for t in (xn[:, :, :, :, NTOK:PADW], q[:, :, :, :, NTOK:PADW], prob[:, :, :, :, NTOK:PADW],
                      vbd[:, :, :, :, :]):
                pool.memset(t, 0.0).then_inc(zeroed, 1)
            pool_scale(pool, 0, 0)

            def image(i, last):
                with pool.Fori(0, 3) as p:
                    pool_scale(pool, i * NWIN + 2 * p + 1, 1)
                    pool_scale(pool, i * NWIN + 2 * p + 2, 0)
                pool_scale(pool, i * NWIN + 7, 1)
                if not last:
                    pool_scale(pool, i * NWIN + 8, 0)

            with pool.Fori(0, B - 1) as i:
                image(i, False)
            image(B - 1, True)

        @block.vector
        def _(dve):
            dve.wait_ge(consts, 16 * NCONST)
            dve.tensor_scalar(bqs[:, :], bqk[:, 0:NC], QSCALE, None, ALU.mult).then_inc(bias_ready, 1)
            dve.tensor_scalar(bkm[:, :], kmask[:, :], bqk[:, 3:4], None, ALU.mult).then_inc(bias_ready, 1)
            for last_row in range(2):
                for p in range(PAIRS):
                    dve.tensor_tensor(bias[:, last_row, p, :, :], rel_sb[:, :, :],
                                      mask_sb[:, last_row, p, :].unsqueeze(1)
                                      .broadcast_to([128, HEADS, NTOK]), ALU.add).then_inc(bias_ready, 1)
            dve.wait_ge(bias_ready, 10)
            dve.wait_ge(zeroed, 4)
            dve.wait_ge(x_loaded, 16)
            stats.rows(dve, 0, range(NWIN))
            stats.aggregate(dve, 0)
            stats.spread(dve, 0)
            stats.variance(dve, 0)
            stats.affine(dve, 0)
            dve_step(dve, -1, 1, attend=False)

            def image(i, last):
                def pair(j0, step_rows=0, last_pair=False):
                    for k in range(2):
                        dve_step(dve, i * NWIN + j0 + k, k, front=not (last and last_pair and k == 1),
                                 last_row=int(last_pair and k == 0),
                                 statistics=i + 1 if last_pair and k == 0 and not last else None)
                        dve_measure(dve, i * NWIN + j0 + k, i, j0 + k)
                        if step_rows is not None and not last:
                            dve.wait_ge(x_loaded, 16 * (i + 2))
                            first = step_rows + 2 * k
                            stats.rows(dve, i + 1, (first, first + 1))

                pair(0, None)
                with dve.Fori(1, 3) as p:
                    pair(2 * p, 4 * p - 4)
                if not last:
                    stats.aggregate(dve, i + 1)
                pair(6, None, True)
                dve_sum_up(dve, i)

            with dve.Fori(0, B - 1) as i:
                image(i, False)
            image(B - 1, True)

        @block.scalar
        def _(act):
            act.wait_ge(zeroed, 4)
            act.wait_ge(bias_ready, 10)
            act.wait_ge(x_loaded, 16)
            stats.root(act, 0)
            act_norm(act, 0, 0, 0)
            act_step(act, -1, 1, attend=False, image=0)

            def image(i, last):
                def pair(j0, last_pair=False):
                    for k in range(2):
                        end = last and last_pair
                        act_step(act, i * NWIN + j0 + k, k, front=not (end and k == 1),
                                 image=None if end else i + 1 if last_pair else i,
                                 statistics=i + 1 if last_pair and k == 0 and not last else None)

                with act.Fori(0, 3) as p:
                    pair(2 * p)
                if not last:
                    act.wait_ge(x_loaded, 16 * (i + 2))
                pair(6, True)

            with act.Fori(0, B - 1) as i:
                image(i, False)
            image(B - 1, True)

        @block.tensor
        def _(pe):
            pe.wait_ge(consts, 16 * NCONST)
            pe.wait_ge(zeroed, 4)
            stats.mean_mm(pe, 0)
            stats.var_mm(pe, 0)
            pe_step(pe, -1, 1, attend=False)

            def image(i, last):
                def pair(j0, last_pair=False):
                    for k in range(2):
                        pe_step(pe, i * NWIN + j0 + k, k, front=not (last and last_pair and k == 1),
                                statistics=i + 1 if last_pair and k == 0 and not last else None)

                with pe.Fori(0, 3) as p:
                    pair(2 * p)
                pair(6, True)

            with pe.Fori(0, B - 1) as i:
                image(i, False)
            image(B - 1, True)


def outlook_layer(nc, x1, mv, out, w_v, w_a, b_a, w_proj, b_proj, gmat_d):
    with ExitStack() as ctx:
        def sb(name, shape):
            return ctx.enter_context(nc.sbuf_tensor(name, shape, F32))

        def sem(name):
            return ctx.enter_context(nc.semaphore(name))

        bank = [ctx.enter_context(nc.psum_tensor(f"l1_bank{i}", [128, 512], F32)) for i in range(8)]
        OB, VB = bank[0:6], bank[6:8]
        IB = 5
        bank_rows = [range(i, min(i + IB, HN)) for i in range(0, HN, IB)]
        NB = len(bank_rows)
        NG = NC * 2
        NH = NG * HC
        PP = KK * KK
        JP = HALF // 2
        PARTS = [range(0, 8), range(8, HALF)]
        SLOTS = 4
        TSLOTS = HC
        ZSLOTS = 2
        ops = NWIN // SLOTS

        rows = sb("rows", [CH, SLOTS, NC, ROW])
        wv = sb("wv", [CH, NC, C])
        wa = sb("wa", [CH, NC, 2 * AH])
        ba = sb("ba", [128, AH])
        wp_sb = sb("wp1", [CH, NC, C])
        bp = sb("bp1", [CH, NC])
        gmat = sb("gmat1", [CH, CH])
        norm = sb("norm1", [CH, 2, B, NC])
        xn = sb("xn1", [CH, 2, NC, 2, RAS, SX])
        y = sb("y", [CH, NC, RAS, RAS])
        rowsum = sb("rowsum", [CH, HALF, 2 * HALF])
        pooled = sb("pooled", [CH, NC, HALF, 2, IP])
        a = sb("a", [128, HALF, AH])
        total = sb("total1", [128, HALF, HC * KK])
        z = sb("z", [CH, ZSLOTS, TC * SX])
        t = sb("t", [CH, TSLOTS, TC * IP])
        v = sb("v", [CH, HN, CH])
        o = sb("o1", [CH, HN, TC])

        consts, zeroed, passed = sem("consts1"), sem("zeroed1"), sem("passed1")
        normed = sem("normed")
        x_loaded = [sem(f"x_loaded{s}") for s in range(SLOTS)]
        res_loaded = [sem(f"res_loaded{s}") for s in range(SLOTS)]
        out_stored = [sem(f"out_stored{s}") for s in range(SLOTS)]
        xn_raw, xn_ready = sem("xn1_raw"), sem("xn1_ready")
        rowsum_ready, pooled_ready = sem("rowsum_ready"), sem("pooled_ready")
        a_raw, a_biased = sem("a_raw"), sem("a_biased")
        top_ready, a_centred, a_exp = sem("top1_ready"), sem("a_centred"), sem("a_exp")
        total_ready, rtotal_ready = sem("total1_ready"), sem("rtotal1_ready")
        a_scaled, a_ready = sem("a_scaled"), sem("a_ready")
        z_begun, z_ready, t_ready = sem("z_begun"), sem("z_ready"), sem("t_ready")
        v_raw, v_ready = sem("v1_raw"), sem("v1_ready")
        o_raw, o_ready = sem("o1_raw"), sem("o1_ready")
        folded, y_ready = sem("folded"), sem("y_ready")
        proj_raw, res_done = sem("proj1_raw"), sem("res1_done")
        NORMS = 2 * NC
        POOLS = NC * 2 * 2
        FOLDED = [0, 3, 8, 11]
        FOLDS = 16


        STATS_PSUM = VB[0][0:CH, 0:B * NC]

        def flat(s):
            return s.rearrange("p i c -> p (i c)")

        def pe_norms(pe):
            pe.matmul(STATS_PSUM, gmat[:, :], flat(mv[:, :, :, 0]), start=True, stop=True).then_inc(normed, 1)
            pe.wait_ge(normed, 5)
            pe.matmul(STATS_PSUM, gmat[:, :], flat(mv[:, :, :, 0]), start=True, stop=True).then_inc(normed, 1)
            pe.wait_ge(normed, 7)

        def dve_norms(dve):
            dve.wait_ge(normed, 1)
            dve.tensor_tensor(flat(mv[:, :, :, 0]), flat(mv[:, :, :, 0]), STATS_PSUM, ALU.subtract) \
                .then_inc(normed, 1)
            dve.tensor_copy(flat(norm[:, 1, :, :]), STATS_PSUM).then_inc(normed, 1)
            dve.wait_ge(normed, 3)
            dve.tensor_tensor(flat(mv[:, :, :, 0]), flat(mv[:, :, :, 0]), flat(mv[:, :, :, 0]), ALU.mult) \
                .then_inc(normed, 1)
            dve.wait_ge(normed, 4)
            dve.tensor_tensor(flat(mv[:, :, :, 0]), flat(mv[:, :, :, 0]), flat(mv[:, :, :, 1]), ALU.add) \
                .then_inc(normed, 1)
            dve.wait_ge(normed, 6)
            dve.tensor_scalar(flat(mv[:, :, :, 0]), STATS_PSUM, GN_EPS, None, ALU.add).then_inc(normed, 1)
            scale, bias = flat(norm[:, 0, :, :]), flat(norm[:, 1, :, :])
            dve.wait_ge(normed, 8)
            dve.reciprocal(scale, flat(mv[:, :, :, 0])).then_inc(normed, 1)
            dve.wait_ge(normed, 9)
            dve.scalar_tensor_tensor(out=bias, in0=bias, scalar=-1.0, in1=scale,
                                     op0=ALU.mult, op1=ALU.mult).then_inc(normed, 1)
            dve.wait_ge(normed, 10)

        def act_norms(act):
            act.wait_ge(normed, 7)
            act.activation(flat(mv[:, :, :, 0]), flat(mv[:, :, :, 0]), ACT.Sqrt).then_inc(normed, 1)
            act.wait_ge(normed, 10)


        def norm_pieces(i, s, row):
            first = WIN * row + SHIFT + 1
            return [(xn[:, s, c, f, first:first + WIN, SHIFT + 1:SX].rearrange("p r (w n) -> p w r n", n=WIN),
                     rows[:, row % SLOTS, c, f * ROW // 2:(f + 1) * ROW // 2]
                     .rearrange("p (w r n) -> p w r n", r=WIN, n=WIN),
                     norm[:, 0, bass.ds(i, 1), c], norm[:, 1, bass.ds(i, 1), c])
                    for c in range(NC) for f in range(2)]

        def dve_norm(dve, i, s, row):
            dve.wait_ge(x_loaded[row % SLOTS], 16 * (ops * i + row // SLOTS + 1))
            if row == 0:
                past(dve, v_raw, NG * NB * (i - 1))
            dve.sem_inc(passed, 1)
            for raster, x, scale, shift in norm_pieces(i, s, row):
                dve.tensor_scalar(raster, x, scale, shift, ALU.mult, ALU.add).then_inc(xn_raw, 1)

        def pool_wrap_xn(pool, i, s):
            pool.wait_ge(xn_raw, NORMS * NWIN * (i + 1))
            pool.sem_inc(passed, 1)
            for c in range(NC):
                pool.tensor_copy(xn[:, s, c, 0, SHIFT + 1:RAS, 1:SHIFT + 1],
                                 xn[:, s, c, 1, SHIFT + 1:RAS, SX - SHIFT:SX]).then_inc(xn_ready, 1)
                pool.tensor_copy(xn[:, s, c, 1, SHIFT + 1:RAS, 0:SHIFT + 1],
                                 xn[:, s, c, 0, SHIFT + 1:RAS, 2 * HALF:SX]).then_inc(xn_ready, 1)
            pool.wait_ge(xn_ready, 6 * i + 4)
            pool.sem_inc(passed, 1)
            for c in range(NC):
                pool.tensor_copy(xn[:, s, c, :, 1:SHIFT + 1, :], xn[:, s, c, :, H + 1:RAS, :]) \
                    .then_inc(xn_ready, 1)

        def dve_pool(dve, i, s, c):
            dve.wait_ge(xn_ready, 6 * (i + 1))
            for n in range(4 * c, 4 * c + 4):
                f, i0 = n // 2 % 2, HALF * (n % 2)
                at(dve, pooled_ready, POOLS * i + n)
                r0, r1 = 1 + 2 * i0, 1 + 2 * (i0 + HALF)
                dve.tensor_tensor(rowsum[:, :, :], xn[:, s, c, f, r0:r1:2, 1:2 * HALF + 1],
                                  xn[:, s, c, f, r0 + 1:r1 + 1:2, 1:2 * HALF + 1], ALU.add) \
                    .then_inc(rowsum_ready, 1)
                dve.wait_ge(rowsum_ready, POOLS * i + n + 1)
                pair = rowsum[:, :, :].rearrange("p i (j b) -> p i j b", b=2)
                dve.tensor_tensor(pooled[:, c, :, f, i0:i0 + HALF].rearrange("p j i -> p i j"),
                                  pair[:, :, :, 0], pair[:, :, :, 1], ALU.add).then_inc(pooled_ready, 1)

        def pe_logits(pe, i):
            pe.wait_ge(pooled_ready, POOLS * (i + 1))
            for jp in range(JP):
                if jp < 2:
                    at(pe, v_ready, NG * NB * i)
                else:
                    pe.wait_ge(a_biased, JP * i + jp - 1)
                for j in range(2):
                    for kc in range(NC):
                        for hc in range(NC):
                            mm = pe.matmul(VB[(jp + 1) % 2][64 * hc:64 * hc + 64, j * AH:(j + 1) * AH],
                                           pooled[:, kc, 2 * jp + j, :, :].rearrange("p f i -> p (f i)"),
                                           wa[:, kc, hc * AH:(hc + 1) * AH], start=(kc == 0), stop=(kc == NC - 1))
                mm.then_inc(a_raw, 1)

        def part(n):
            return a[:, PARTS[n].start:PARTS[n].stop, :].rearrange("P j (x q) -> P (j x) q", q=KK)

        def of_part(n):
            return total[:, PARTS[n].start:PARTS[n].stop, :].rearrange("P j x -> P (j x)")

        def dve_logits(dve, i, jp):
            if jp == 0:
                at(dve, z_ready, K * NH * i)
            dve.wait_ge(a_raw, JP * i + jp + 1)
            dve.scalar_tensor_tensor(out=a[:, 2 * jp:2 * jp + 2, :],
                                     in0=VB[(jp + 1) % 2][:, 0:2 * AH].rearrange("p (j a) -> p j a", j=2),
                                     scalar=0.25, in1=ba[:, :].unsqueeze(1).broadcast_to([128, 2, AH]),
                                     op0=ALU.mult, op1=ALU.add).then_inc(a_biased, 1)

        def dve_top(dve, i, n):
            dve.wait_ge(a_biased, JP * i + PARTS[n].stop // 2)
            at(dve, a_scaled, HC * i)
            dve.tensor_reduce(of_part(n), part(n), AX.X, ALU.max).then_inc(top_ready, 1)

        def dve_centre(dve, i, n):
            dve.wait_ge(top_ready, 2 * i + n + 1)
            top = of_part(n).unsqueeze(2).broadcast_to([128, len(PARTS[n]) * HC * KK, KK])
            dve.tensor_tensor(part(n), part(n), top, ALU.subtract).then_inc(a_centred, 1)

        def act_exp(act, i, n):
            act.wait_ge(a_centred, 2 * i + n + 1)
            act.activation(part(n), part(n), ACT.Exp, scale=QSCALE).then_inc(a_exp, 1)

        def dve_total(dve, i, n):
            dve.wait_ge(a_exp, 2 * i + n + 1)
            dve.tensor_reduce(of_part(n), part(n), AX.X, ALU.add).then_inc(total_ready, 1)
            dve.wait_ge(total_ready, 2 * i + n + 1)
            dve.reciprocal(of_part(n), of_part(n)).then_inc(rtotal_ready, 1)

        def dve_softmax(dve, i):
            for jp in range(JP):
                dve_logits(dve, i, jp)
                if jp == 3:
                    dve_top(dve, i, 0)
                if jp == 4:
                    dve_centre(dve, i, 0)
            dve_top(dve, i, 1)
            dve_centre(dve, i, 1)
            dve_total(dve, i, 0)
            dve_total(dve, i, 1)

        def pool_scale(pool, i, h):
            pool.wait_ge(rtotal_ready, 2 * (i + 1))
            head = a[:, :, h * PP:(h + 1) * PP].rearrange("P j (p q) -> P j p q", q=KK)
            pool.tensor_tensor(head, head, total[:, :, h * KK:(h + 1) * KK].unsqueeze(3)
                               .broadcast_to([128, HALF, KK, KK]), ALU.mult).then_inc(a_scaled, 1)
            first = h * PP
            left = a[:, 0:HALF - 1, first + 2 * K * KK + K - 1:first + KK * KK:K]
            right = a[:, 1:HALF, first:first + K * KK:K]
            pool.wait_ge(a_scaled, HC * i + h + 1)
            pool.tensor_tensor(left, left, right, ALU.add).then_inc(a_ready, 1)

        def act_spread(act, i, hs):
            g, h = hs // HC, hs % HC
            act.wait_ge(a_ready, HC * i + h + 1)
            at(act, t_ready, NH * i + hs + 1 - ZSLOTS)
            for p0, p1 in ((0, 2 * K), (2 * K, KK)):
                if p0:
                    act.wait_ge(z_begun, K * (NH * i + hs + 1))
                for qy in range(K):
                    first = z[32 * qy:32 * qy + 32, hs % ZSLOTS, p0 * SX:p0 * SX + 1]
                    diagonal = bass.AP(first.tensor, first.offset,
                                       [[first.ap[0][0], 32], [SX, p1 - p0], [2 * K * SX + 2, HALF], [1, K]])
                    src = a[32 * g:32 * g + 32, :, h * PP:(h + 1) * PP].rearrange(
                        "P j (p u v) -> P u p j v", u=K, v=K)[:, qy, p0:p1, :, :]
                    act.activation(diagonal, src, ACT.Copy).then_inc(z_ready if p0 else z_begun, 1)

        def dve_turn(dve, i, hs):
            dve.wait_ge(z_ready, K * (NH * i + hs + 1))
            past(dve, o_raw, NB * (NG * i + hs // HC))
            dve.transpose(t[:, hs % TSLOTS, :], z[:, hs % ZSLOTS, :]).then_inc(t_ready, 1)

        def pe_values(pe, i, g, s):
            c, f = g // 2, g % 2
            for kb in range(NB):
                if g == 0 and kb < 2:
                    pe.wait_ge(a_biased, JP * (i + 1) - 1 + kb)
                at(pe, v_ready, NB * (NG * i + g) + kb - 1)
                for k, row in enumerate(bank_rows[kb]):
                    for kc in range(NC):
                        mm = pe.matmul(VB[kb % 2][0:CH, k * CH:(k + 1) * CH],
                                       xn[:, s, kc, f, 2 * row:2 * row + K, :].rearrange("p r x -> p (r x)"),
                                       wv[:, kc, c * CH:(c + 1) * CH], start=(kc == 0), stop=(kc == NC - 1))
                mm.then_inc(v_raw, 1)

        def act_values(act, i, g, kb):
            past(act, v_raw, NB * (NG * i + g) + kb + 1)
            r = bank_rows[kb]
            act.activation(v[:, r.start:r.stop, :].rearrange("p i d -> p (i d)"),
                           VB[kb % 2][0:CH, 0:len(r) * CH], ACT.Copy).then_inc(v_ready, 1)

        def pe_heads(pe, i, g):
            pe.wait_ge(t_ready, NH * i + HC * (g + 1))
            if g == 0:
                past(pe, res_done, 2 * NWIN * i)
            for kb in range(NB):
                pe.wait_ge(v_ready, NB * (NG * i + g) + kb + 1)
                if g > 0:
                    pe.wait_ge(o_ready, NB * (NG * i + g - 1) + kb + 1)
                for k, row in enumerate(bank_rows[kb]):
                    for h in range(HC):
                        turned = t[:, (HC * g + h) % TSLOTS, :].rearrange("p (n i) -> p n i", i=IP)
                        mm = pe.matmul(OB[kb][32 * h:32 * h + 32, k * TC:(k + 1) * TC],
                                       v[:, row, HD * h:HD * (h + 1)], turned[:, :, row],
                                       start=True, stop=True)
                mm.then_inc(o_raw, 1)

        def act_outputs(act, i, g, kb):
            past(act, o_raw, NB * (NG * i + g) + kb + 1)
            past(act, folded, FOLDS * i + FOLDED[g])
            r = bank_rows[kb]
            act.activation(o[:, r.start:r.stop, :].rearrange("p i n -> p (i n)"),
                           OB[kb][0:CH, 0:len(r) * TC], ACT.Copy).then_inc(o_ready, 1)

        def pool_fold(pool, i, g):
            c, f = g // 2, g % 2
            pool.wait_ge(o_ready, NB * (NG * i + g + 1))
            if g == 0:
                past(pool, proj_raw, 2 * NWIN * i)
            pool.sem_inc(passed, 1)
            out = o[:, :, :].rearrange("p i (x r) -> p i x r", r=K)
            steps = [(1, 1, XT, False), (2, 1, XT, False)]
            if f == 1:
                steps += [(1, 0, 1, True), (2, 0, 1, True)]
            steps += [(0, 1 - f, XT, True)]
            for n, (py, x0, x1_, add) in enumerate(steps):
                i0 = 1 if py == 0 else 0
                r0 = 2 * i0 + py
                dst = y[:, c, r0:r0 + 2 * (HN - i0) - 1:2, 2 * HALF * f + x0:2 * HALF * f + x1_]
                src = out[:, i0:HN, x0:x1_, py]
                if add:
                    past(pool, folded, FOLDS * i + FOLDED[g] + n)
                    pool.tensor_tensor(dst, dst, src, ALU.add).then_inc(folded, 1)
                else:
                    pool.tensor_copy(dst, src).then_inc(folded, 1)

        def pool_wrap_y(pool, i):
            past(pool, folded, FOLDS * (i + 1))
            pool.sem_inc(passed, 1)
            for c in range(NC):
                pool.tensor_copy(y[:, c, 1:H + 1, W + 1:RAS], y[:, c, 1:H + 1, 1:SHIFT + 1]).then_inc(y_ready, 1)
            pool.wait_ge(y_ready, 4 * i + 2)
            pool.sem_inc(passed, 1)
            for c in range(NC):
                pool.tensor_copy(y[:, c, H + 1:RAS, 1:RAS], y[:, c, 1:SHIFT + 1, 1:RAS]).then_inc(y_ready, 1)

        def proj_bank(row, c):
            return OB[2 * (row % 3) + c][0:CH, 0:ROW]

        def pe_proj(pe, i):
            pe.wait_ge(y_ready, 4 * (i + 1))
            for row in range(NWIN):
                if row >= 3:
                    past(pe, res_done, 2 * (NWIN * i + row - 2))
                first = WIN * row + SHIFT + 1
                for c in range(NC):
                    for kc in range(NC):
                        mm = pe.matmul(proj_bank(row, c), wp_sb[:, kc, c * CH:(c + 1) * CH],
                                       y[:, kc, first:first + WIN, SHIFT + 1:RAS]
                                       .rearrange("p r (w n) -> p w r n", n=WIN),
                                       start=(kc == 0), stop=(kc == NC - 1))
                    mm.then_inc(proj_raw, 1)

        def dve_residual(dve, i, row):
            dve.wait_ge(res_loaded[row % SLOTS], 16 * (ops * i + row // SLOTS + 1))
            for c in range(NC):
                past(dve, proj_raw, 2 * (NWIN * i + row) + c + 1)
                r = rows[:, row % SLOTS, c, :]
                dve.scalar_tensor_tensor(out=r, in0=proj_bank(row, c), scalar=bp[:, c:c + 1], in1=r,
                                         op0=ALU.add, op1=ALU.add).then_inc(res_done, 1)

        block = ctx.enter_context(nc.Block())

        def images(engine, image):
            with engine.Fori(0, B // 2 - 1) as pair:
                for s in range(2):
                    image(2 * pair + s, s, False)
            image(B - 2, 0, False)
            image(B - 1, 1, True)

        @block.sync
        def _(sp):
            for src, dst in ((w_v, wv[:, :, :]), (w_a, wa[:, :, :]), (w_proj, wp_sb[:, :, :]),
                             (b_proj, bp[:, :]), (gmat_d, gmat[:, :]),
                             (b_a[0:1, :].broadcast_to([64, AH]), ba[0:64, :]),
                             (b_a[1:2, :].broadcast_to([64, AH]), ba[64:128, :])):
                sp.dma_start(dst, src).then_inc(consts, 16)

            def dram_row(dram, i, row):
                return dram[bass.ds(i, 1), :, NC * ROW * row:NC * ROW * (row + 1)].rearrange("a p n -> (a p) n")

            def ring(row):
                return rows[:, row % SLOTS, :, :].rearrange("p c n -> p (c n)")

            def load_for_norm(i):
                for row in range(NWIN):
                    if row < SLOTS:
                        past(sp, out_stored[row], 16 * ops * (i - 1))
                    else:
                        sp.wait_ge(xn_raw, NORMS * (NWIN * i + row - SLOTS + 1))
                    sp.dma_start(ring(row), dram_row(x1, i, row)).then_inc(x_loaded[row % SLOTS], 16)

            def load_for_residual(i, row):
                sp.dma_start(ring(row), dram_row(x1, i, row)).then_inc(res_loaded[row % SLOTS], 16)

            def wait_stored(i, row):
                past(sp, out_stored[row % SLOTS], 16 * (ops * i + row // SLOTS + 1))

            def image(i, s, last):
                if not last:
                    load_for_norm(i + 1)
                for row in range(SLOTS):
                    if last:
                        past(sp, out_stored[row], 16 * ops * i)
                    else:
                        sp.wait_ge(xn_raw, NORMS * (NWIN * (i + 1) + SLOTS + row + 1))
                    load_for_residual(i, row)
                for row in range(NWIN):
                    past(sp, res_done, 2 * (NWIN * i + row + 1))
                    sp.dma_start(dram_row(out, i, row), ring(row)).then_inc(out_stored[row % SLOTS], 16)
                    if 1 <= row <= SLOTS:
                        wait_stored(i, row - 1)
                        load_for_residual(i, row - 1 + SLOTS)
                if last:
                    for row in range(SLOTS, NWIN):
                        wait_stored(i, row)

            load_for_norm(0)
            sp.wait_ge(xn_raw, NORMS * NWIN)
            images(sp, image)

        @block.gpsimd
        def _(pool):
            start_at_one(pool, o_raw, v_raw, folded, proj_raw, res_done, *out_stored)
            for t0 in (xn[:, :, :, :, :, :], pooled[:, :, :, :, :], z[:, :, :], y[:, :, :, :]):
                pool.memset(t0, 0.0).then_inc(zeroed, 1)
            pool_wrap_xn(pool, 0, 0)
            for h in range(HC):
                pool_scale(pool, 0, h)

            def image(i, s, last):
                for g in range(NG):
                    if g == 1 and not last:
                        pool_wrap_xn(pool, i + 1, 1 - s)
                    pool_fold(pool, i, g)
                pool_wrap_y(pool, i)
                if not last:
                    for h in range(HC):
                        pool_scale(pool, i + 1, h)

            images(pool, image)

        @block.vector
        def _(dve):
            dve.wait_ge(consts, 16 * 7)
            dve.wait_ge(zeroed, 4)
            dve_norms(dve)
            for row in range(NWIN):
                dve_norm(dve, 0, 0, row)
            for c in range(NC):
                dve_pool(dve, 0, 0, c)
            dve_softmax(dve, 0)
            for hs in range(HC):
                dve_turn(dve, 0, hs)

            def image(i, s, last):
                for g in range(NG):
                    if not last and g < 2:
                        for row in range(SLOTS * g, SLOTS * (g + 1)):
                            dve_norm(dve, i + 1, 1 - s, row)
                    if not last and g >= 2:
                        dve_pool(dve, i + 1, 1 - s, g - 2)
                    if g < NG - 1:
                        for h in range(HC):
                            dve_turn(dve, i, HC * (g + 1) + h)
                if not last:
                    dve_softmax(dve, i + 1)
                for row in range(NWIN):
                    dve_residual(dve, i, row)
                    if not last and row in (1, 3, 5):
                        dve_turn(dve, i + 1, row // 2)

            images(dve, image)

        @block.scalar
        def _(act):
            act.wait_ge(zeroed, 4)
            act_norms(act)

            def begin(i):
                act_exp(act, i, 0)
                act_values(act, i, 0, 0)
                act_values(act, i, 0, 1)
                act_exp(act, i, 1)
                for kb in range(2, NB):
                    act_values(act, i, 0, kb)
                act_spread(act, i, 0)
                act_spread(act, i, 1)
                act_spread(act, i, 2)

            begin(0)

            def image(i, s, last):
                act_spread(act, i, HC)
                for g in range(NG):
                    more = g < NG - 1
                    nxt = HC * (g + 1)
                    if more:
                        act_spread(act, i, nxt + 1)
                    for kb in range(NB):
                        act_outputs(act, i, g, kb)
                    if more:
                        for kb in range(NB):
                            act_values(act, i, g + 1, kb)
                            if kb == 1:
                                act_spread(act, i, nxt + 2)
                            if kb == 3 and g < NG - 2:
                                act_spread(act, i, nxt + HC)
                if not last:
                    begin(i + 1)

            images(act, image)

        @block.tensor
        def _(pe):
            pe.wait_ge(consts, 16 * 7)
            pe.wait_ge(zeroed, 4)
            pe_norms(pe)
            pe_logits(pe, 0)
            pe_values(pe, 0, 0, 0)

            def image(i, s, last):
                for g in range(NG):
                    pe_heads(pe, i, g)
                    if g < NG - 1:
                        pe_values(pe, i, g + 1, s)
                if not last:
                    pe_logits(pe, i + 1)
                    pe_values(pe, i + 1, 0, 1 - s)
                pe_proj(pe, i)

            images(pe, image)


def preact_block(nc, x, w_qkv, b_qk, b_v, w_proj, b_proj, rel, mask, gmat, kmask, ident, w_v, w_a, b_a,
                 w_proj1, b_proj1, out):
    x1 = nc.dram_tensor("x1_scratch", [B, CH, NWIN * NC * ROW], F32, kind="Internal").ap()
    with nc.sbuf_tensor("mv1", [CH, B, NC, 2], F32) as mv1:
        window_layer(nc, x, x1, mv1, w_qkv, b_qk, b_v, w_proj, b_proj, rel, mask, gmat, kmask, ident)
        outlook_layer(nc, x1, mv1, out, w_v, w_a, b_a, w_proj1, b_proj1, gmat)



def shift_mask():
    region = np.zeros((H, W), np.float32)
    cuts = ((0, H - WIN), (H - WIN, H - SHIFT), (H - SHIFT, H))
    for n, (h0, h1) in enumerate(cuts):
        for m, (w0, w1) in enumerate(cuts):
            region[h0:h1, w0:w1] = 3 * n + m
    win = region.reshape(NWIN, WIN, NWIN, WIN).transpose(0, 2, 1, 3).reshape(NWIN, NWIN, NTOK)
    out = np.zeros((2, PADW, 2, PAIRS, NTOK), np.float32)
    for last_row, wy in enumerate((0, NWIN - 1)):
        for wx in range(NWIN):
            differ = win[wy, wx][:, None] != win[wy, wx][None, :]
            out[wx % 2, :NTOK, last_row, wx // 2] = np.where(differ, np.float32(-100), np.float32(0))
    return out.reshape(128, 2, PAIRS, NTOK)


def rel_index():
    coords = np.stack(np.meshgrid(np.arange(WIN), np.arange(WIN), indexing="ij")).reshape(2, -1)
    rel = coords[:, :, None] - coords[:, None, :] + WIN - 1
    return rel[0] * (2 * WIN - 1) + rel[1]


def column_first(w):
    w = w.reshape(-1, HEADS, K, K, KK).transpose(0, 1, 3, 2, 4)
    return np.ascontiguousarray(w.reshape(-1, HEADS * KK * KK))



def to_windows(x):
    x = np.roll(x, (-SHIFT, -SHIFT), axis=(1, 2))
    x = x.reshape(B, NWIN, WIN, NWIN, WIN, NC, CH).transpose(0, 6, 1, 5, 3, 2, 4)
    return np.ascontiguousarray(x.reshape(B, CH, NWIN * NC * ROW))


def from_windows(x):
    x = x.reshape(B, CH, NWIN, NC, NWIN, WIN, WIN).transpose(0, 2, 5, 4, 6, 3, 1)
    return np.ascontiguousarray(np.roll(x.reshape(B, H, W, C), (SHIFT, SHIFT), axis=(1, 2)))


def kernel(**inputs):
    import concourse.bacc as _bacc
    from concourse.bass_utils import run_bass_kernel_spmd as _run

    a = {k: np.asarray(v) for k, v in inputs.items()}

    def chunked(w):
        return np.ascontiguousarray(w.reshape(NC, CH, -1).transpose(1, 0, 2))

    qkv_b = a["L0_conv_qkv_bias"]
    b_v = np.zeros((128, 2), np.float32)
    b_v[:, 0] = qkv_b[2 * C:2 * C + 128]
    b_v[0:64, 1] = qkv_b[2 * C + 128:]
    rel = np.zeros((2, PADW, HEADS, NTOK), np.float32)
    rel[:, :NTOK] = a["L0_conv_rel_bias_table"][rel_index()].transpose(0, 2, 1)[None]
    arrays = {
        "x": to_windows(a["x"]),
        "w_qkv": chunked(a["L0_conv_qkv_weight"].T),
        "b_qk": np.ascontiguousarray(qkv_b[:2 * C].reshape(4, CH).T),
        "b_v": b_v,
        "w_proj": np.ascontiguousarray(a["L0_conv_proj_weight"].T),
        "b_proj": np.ascontiguousarray(a["L0_conv_proj_bias"].reshape(NC, CH).T),
        "rel": rel.reshape(128, HEADS, NTOK),
        "mask": shift_mask(),
        "gmat": np.kron(np.eye(CH // GC), np.full((GC, GC), 1.0 / GC)).astype(np.float32),
        "kmask": np.kron(np.eye(HC), np.ones((HD, 1))).astype(np.float32),
        "ident": np.eye(128, dtype=np.float32),
        "w_v": chunked(a["L1_conv_Wv"]),
        "w_a": chunked(column_first(a["L1_conv_Wa"])),
        "b_a": column_first(a["L1_conv_ba"]).reshape(NC, AH),
        "w_proj1": chunked(a["L1_conv_Wp"]),
        "b_proj1": np.ascontiguousarray(a["L1_conv_bp"].reshape(NC, CH).T),
    }
    nc = _bacc.Bacc("TRN2", target_bir_lowering=False, num_devices=1)
    aps = [nc.dram_tensor("in_" + name, v.shape, F32, kind="ExternalInput").ap() for name, v in arrays.items()]
    out = nc.dram_tensor("out", [B, CH, NWIN * NC * ROW], F32, kind="ExternalOutput").ap()
    preact_block(nc, *aps, out)
    r = _run(nc, [{"in_" + k: v for k, v in arrays.items()}], core_ids=[0])
    return from_windows(r.results[0]["out"])
```

```python
from contextlib import ExitStack

import numpy as np
import concourse.bass as bass
from concourse import mybir

F32 = mybir.dt.float32
ALU = mybir.AluOpType
ACT = mybir.ActivationFunctionType
AX = mybir.AxisListType

B, H, W, C = 32, 56, 56, 192
HEADS, HD = 6, 32
WIN, SHIFT = 7, 3
NTOK = WIN * WIN
NWIN = H // WIN
ROW = NWIN * NTOK
CH = 96
NC = C // CH
HC = HEADS // NC
GROUPS = 32
GC = C // GROUPS
GN_EPS = 1e-5
PADW = 64
PAIRS = NWIN // 2
QSCALE = HD ** -0.5
QH = 128 // HD
RH = HEADS - QH
K = 3
KK = K * K
HN = H // 2
HALF = HN // 2
SX = 32
IP = 32
RAS = 60
XT = 2 * HALF + 1
TC = K * XT
AH = HC * KK * KK
BN = 6
STAT_STEPS = 16 + 2 + 4 + 3


def at(eng, sem, value):
    if isinstance(value, int) and value <= 0:
        return
    eng.wait_ge(sem, value)




def past(eng, sem, value):
    at(eng, sem, value + 1)


def start_at_one(eng, *sems):
    for s in sems:
        eng.sem_inc(s, 1)


class Stats:

    def __init__(self, sb, sem, tag, psum, gmat, x_row, passed):
        self.bn = sb("bn_" + tag, [CH, NC, NWIN, BN])
        self.mv = sb("mv_" + tag, [CH, NC, 2])
        self.dev = sb("dev_" + tag, [CH, NC])
        self.gmean = sb("gmean_" + tag, [CH, NC])
        self.norm = sb("norm_" + tag, [CH, 2, 2, NC])
        self.var = sb("var_" + tag, [CH, NC])
        self.std = sb("std_" + tag, [CH, NC])
        self.rooted = sem("rooted_" + tag)
        self.passed = passed
        self.step = sem("stat_step_" + tag)
        self.mm = sem("stat_mm_" + tag)
        self.psum, self.gmat, self.x_row = psum, gmat, x_row

    def rows(self, dve, i, rows):
        for row in rows:
            for c in range(NC):
                out = self.bn[:, c, bass.ds(row, 1), :].rearrange("p a n -> p (a n)")
                dve.bn_stats(out, self.x_row(i, row, c)).then_inc(self.step, 1)

    def aggregate(self, dve, i):
        dve.wait_ge(self.step, i * STAT_STEPS + 16)
        dve.sem_inc(self.passed, 1)
        for c in range(NC):
            dve.bn_aggr(self.mv[:, c, :], self.bn[:, c, :, :].rearrange("p a b -> p (a b)")) \
                .then_inc(self.step, 1)

    def mean_mm(self, pe, i):
        pe.wait_ge(self.step, i * STAT_STEPS + 18)
        pe.matmul(self.psum[:, 0:NC], self.gmat[:, :], self.mv[:, :, 0], start=True, stop=True) \
            .then_inc(self.mm, 1)

    def spread(self, dve, i):
        dve.wait_ge(self.mm, 2 * i + 1)
        dve.tensor_tensor(self.dev[:, :], self.mv[:, :, 0], self.psum[:, 0:NC], ALU.subtract) \
            .then_inc(self.step, 1)
        dve.tensor_copy(self.gmean[:, :], self.psum[:, 0:NC]).then_inc(self.step, 1)
        dve.wait_ge(self.step, i * STAT_STEPS + 20)
        dve.tensor_tensor(self.dev[:, :], self.dev[:, :], self.dev[:, :], ALU.mult) \
            .then_inc(self.step, 1)
        dve.wait_ge(self.step, i * STAT_STEPS + 21)
        dve.tensor_tensor(self.dev[:, :], self.dev[:, :], self.mv[:, :, 1], ALU.add) \
            .then_inc(self.step, 1)

    def var_mm(self, pe, i):
        pe.wait_ge(self.step, i * STAT_STEPS + 22)
        pe.matmul(self.psum[:, 0:NC], self.gmat[:, :], self.dev[:, :], start=True, stop=True) \
            .then_inc(self.mm, 1)

    def variance(self, dve, i):
        dve.wait_ge(self.mm, 2 * i + 2)
        dve.tensor_scalar(self.var[:, :], self.psum[:, 0:NC], GN_EPS, None, ALU.add).then_inc(self.step, 1)

    def root(self, act, i):
        act.wait_ge(self.step, i * STAT_STEPS + 23)
        act.activation(self.std[:, :], self.var[:, :], ACT.Sqrt).then_inc(self.rooted, 1)

    def affine(self, dve, i):
        scale = self.norm[:, bass.ds(i % 2, 1), 0, :].rearrange("p a c -> p (a c)")
        bias = self.norm[:, bass.ds(i % 2, 1), 1, :].rearrange("p a c -> p (a c)")
        dve.wait_ge(self.rooted, i + 1)
        dve.reciprocal(scale, self.std[:, :]).then_inc(self.step, 1)
        dve.wait_ge(self.step, i * STAT_STEPS + 24)
        dve.scalar_tensor_tensor(out=bias, in0=self.gmean[:, :], scalar=-1.0, in1=scale,
                                 op0=ALU.mult, op1=ALU.mult).then_inc(self.step, 1)

    def affine_of(self, i, c):
        return (self.norm[:, bass.ds(i % 2, 1), 0, c], self.norm[:, bass.ds(i % 2, 1), 1, c])


def window_layer(nc, x_in, x1, mv1, w_qkv, w_proj, b_proj, rel, mask, gmat_d, kmask_d, ident_d):
    with ExitStack() as ctx:
        def sb(name, shape):
            return ctx.enter_context(nc.sbuf_tensor(name, shape, F32))

        def sem(name):
            return ctx.enter_context(nc.semaphore(name))

        bank = [ctx.enter_context(nc.psum_tensor(f"l0_bank{i}", [128, 512], F32)) for i in range(8)]
        QK, VB, PT, OB = bank[0:2], bank[2], bank[5:7], bank[7]
        SB = bank[3:5]

        x = sb("x", [CH, 2 * NWIN, NC, ROW])
        wqkv = sb("wqkv", [CH + 1, NC, 3 * C])
        wp_sb = sb("wp_sb", [128, 2, C])
        bp = sb("bp", [CH, NC])
        gmat = sb("gmat", [CH, CH])
        kmask = sb("kmask", [128, QH])
        ident = sb("ident", [128, 128])
        rel_sb = sb("rel_sb", [128, HEADS, NTOK])
        mask_sb = sb("mask_sb", [128, 2, PAIRS, NTOK])
        bias = sb("bias", [128, 2, PAIRS, HEADS, NTOK])
        xn = sb("xn", [CH + 1, 2, NC, NWIN, PADW])
        q = sb("q", [128, 2, NWIN, PADW])
        kbd = sb("kbd", [128, 2, QH, ROW])
        q_rest = sb("q_rest", [64, 2, NWIN, PADW])
        kbd_rest = sb("kbd_rest", [64, 2, RH, ROW])
        vbd = sb("vbd", [128, 2, NWIN, 3, 2 * HD])
        logit = sb("logit", [128, PAIRS, HEADS, NTOK])
        prob = sb("prob", [128, 2, PAIRS, HEADS, PADW])
        top = sb("top", [128, PAIRS * HEADS])
        total = sb("total", [128, PAIRS * HEADS])
        rtotal = sb("rtotal", [128, PAIRS * HEADS])
        pt = sb("pt", [128, 2, 3, 128])
        o = sb("o", [128, 2, 2, ROW])
        aggregate = sb("aggregate", [CH, NC, 2])
        bn1 = sb("bn1", [CH, NC, NWIN, BN])

        consts = sem("consts")
        zeroed = sem("zeroed")
        bias_ready = sem("bias_ready")
        x_loaded = sem("x_loaded")
        x_stored = sem("x_stored")
        xn_ready = sem("xn_ready")
        qk_raw = sem("qk_raw")
        q_ready, k_ready, rest_ready = sem("q_ready"), sem("k_ready"), sem("rest_ready")
        v_raw, v_ready = sem("v_raw"), [sem("v_first"), sem("v_second")]
        s_raw, s_biased = sem("s_raw"), sem("s_biased")
        top_ready, centred = sem("top_ready"), sem("centred")
        exp_ready, total_ready, rtotal_ready = sem("exp_ready"), sem("total_ready"), sem("rtotal_ready")
        prob_ready = sem("prob_ready")
        pt_raw, pt_ready = sem("pt_raw"), sem("pt_ready")
        pv_done = sem("pv_done")
        o_raw, o_ready = sem("o_raw"), sem("o_ready")
        proj_raw, res_done = sem("proj_raw"), [sem("res_first"), sem("res_second")]
        measured, summed_up = sem("measured"), sem("summed_up")

        NCONST, ZEROED = 9, 7
        stats = Stats(sb, sem, "l0", OB[0:CH, :], gmat,
                      lambda i, row, c: x[:, bass.ds((i * NWIN + row) % (2 * NWIN), 1), c, :]
                      .rearrange("p a n -> p (a n)"), sem("passed"))

        def x_row(r, c):
            return x[:, bass.ds(r % (2 * NWIN), 1), c, :].rearrange("p a (w n) -> p (a w) n", n=NTOK)


        def act_norm(act, r, i, s):
            at(act, stats.step, (i + 1) * STAT_STEPS)
            at(act, v_raw, 2 * (r - 1))
            for c in range(NC):
                scale, shift = stats.affine_of(i, c)
                act.activation(xn[0:CH, s, c, :, 0:NTOK], x_row(r, c), ACT.Identity, bias=shift,
                               scale=scale).then_inc(xn_ready, 1)

        def pe_qk(pe, r, s):
            pe.wait_ge(xn_ready, 2 * (r + 1))
            for n in range(3):
                if n < 2:
                    past(pe, res_done[n], r - 1)
                else:
                    pe.wait_ge(q_ready, r + 1)
                for kc in range(NC):
                    rows = CH + kc
                    mm = pe.matmul(QK[n % 2][:, 0:ROW], wqkv[0:rows, kc, n * 128:(n + 1) * 128],
                                   xn[0:rows, s, kc, :, 0:NTOK], start=(kc == 0), stop=(kc == NC - 1))
                mm.then_inc(qk_raw, 1)

        def windows(s2):
            return s2.rearrange("p (w n) -> p w n", n=NTOK)

        def act_q(act, r, s):
            past(act, s_raw, 2 * (r - 1))
            act.wait_ge(qk_raw, 3 * r + 1)
            act.activation(q[:, s, :, 0:NTOK], windows(QK[0][:, 0:ROW]), ACT.Copy, scale=QSCALE) \
                .then_inc(q_ready, 1)
            act.wait_ge(qk_raw, 3 * r + 3)
            act.activation(q_rest[:, s, :, 0:NTOK], windows(QK[0][0:64, 0:ROW]), ACT.Copy, scale=QSCALE) \
                .then_inc(rest_ready, 1)
            for h in range(RH):
                act.activation(kbd_rest[HD * h:HD * (h + 1), s, h, :],
                               QK[0][64 + HD * h:64 + HD * (h + 1), 0:ROW], ACT.Copy).then_inc(rest_ready, 1)

        def dve_k(dve, r, s):
            past(dve, s_raw, 2 * (r - 1))
            dve.wait_ge(qk_raw, 3 * r + 2)
            dve.tensor_tensor(kbd[:, s, :, :], QK[1][:, 0:ROW].unsqueeze(1).broadcast_to([128, QH, ROW]),
                              kmask[:, :].unsqueeze(2).broadcast_to([128, QH, ROW]), ALU.mult) \
                .then_inc(k_ready, 1)

        def pe_v(pe, r, s, half):
            at(pe, v_ready[1 - half], 4 * (r + half))
            for p in range(2):
                for kc in range(NC):
                    rows = CH + kc
                    mm = pe.matmul(VB[:, p * C:(p + 1) * C],
                                   xn[0:rows, s, kc, 4 * half + 2 * p:4 * half + 2 * p + 2, :]
                                   .rearrange("p w n -> p (w n)"),
                                   wqkv[0:rows, kc, 2 * C:3 * C], start=(kc == 0), stop=(kc == NC - 1))
            mm.then_inc(v_raw, 1)


        def v_pieces(s, half):
            return [(vbd[64 * odd:64 * odd + 64, s, 4 * half + w:4 * half + w + 3:2, :, odd * HD:(odd + 1) * HD],
                     VB[64 * w:64 * w + 64, 0:2 * C].rearrange("p (a h o d) -> p a h o d", a=2, h=3, o=2)
                     [:, :, :, odd, :]) for w in range(2) for odd in range(2)]

        def dve_v(dve, r, s):
            past(dve, pv_done, 4 * (r - 1))
            dve.wait_ge(v_raw, 2 * r + 1)
            for dst, values in v_pieces(s, 0):
                dve.tensor_copy(dst, values).then_inc(v_ready[0], 1)

        def act_v(act, r, s):
            past(act, pv_done, 4 * (r - 1))
            act.wait_ge(v_raw, 2 * r + 2)
            for dst, values in v_pieces(s, 1):
                act.activation(dst, values, ACT.Copy).then_inc(v_ready[1], 1)

        def pe_logits(pe, r, s, half):
            pe.wait_ge(k_ready, r + 1)
            pe.wait_ge(rest_ready, (1 + RH) * (r + 1))
            at(pe, s_biased, 2 * r + half)
            for p in range(2):
                for w in range(2):
                    win = 4 * half + 2 * p + w
                    rows, keys = slice(64 * w, 64 * w + 64), slice(win * NTOK, (win + 1) * NTOK)
                    pe.matmul(SB[p][rows, 0:QH * NTOK], q[:, s, win, :], kbd[:, s, :, keys],
                              start=True, stop=True)
                    mm = pe.matmul(SB[p][rows, QH * NTOK:HEADS * NTOK], q_rest[:, s, win, :],
                                   kbd_rest[:, s, :, keys], start=True, stop=True)
            mm.then_inc(s_raw, 1)

        def dve_bias(dve, r, half, last_row):
            past(dve, s_raw, 2 * r + half + 1)
            at(dve, exp_ready, r)
            for p in range(2):
                add = dve.tensor_tensor(
                    logit[:, 2 * half + p, :, :].rearrange("p h m -> p (h m)"),
                    SB[p][:, 0:HEADS * NTOK],
                    bias[:, last_row, 2 * half + p, :, :].rearrange("p h m -> p (h m)"), ALU.add)
            add.then_inc(s_biased, 1)

        def half_of(s4, half):
            return s4[:, 2 * half:2 * half + 2, :, 0:NTOK].rearrange("p a h m -> p (a h) m")

        def dve_centre(dve, r, half):
            first, n = half * 2 * HEADS, 2 * HEADS
            dve.wait_ge(s_biased, 2 * r + half + 1)
            dve.tensor_reduce(top[:, first:first + n], half_of(logit, half), AX.X, ALU.max) \
                .then_inc(top_ready, 1)
            dve.wait_ge(top_ready, 2 * r + half + 1)
            dve.tensor_tensor(half_of(logit, half), half_of(logit, half),
                              top[:, first:first + n].unsqueeze(2).broadcast_to([128, n, NTOK]),
                              ALU.subtract).then_inc(centred, 1)

        def act_exp(act, r, s):
            act.wait_ge(centred, 2 * (r + 1))
            past(act, pt_raw, 4 * (r - 1))
            act.activation(prob[:, s, :, :, 0:NTOK].rearrange("p a h m -> p (a h) m"),
                           logit[:, :, :, :].rearrange("p a h m -> p (a h) m"), ACT.Exp) \
                .then_inc(exp_ready, 1)

        def dve_total(dve, r, s):
            dve.wait_ge(exp_ready, r + 1)
            at(dve, prob_ready, r)
            dve.tensor_reduce(total[:, :], prob[:, s, :, :, 0:NTOK].rearrange("p a h m -> p (a h) m"),
                              AX.X, ALU.add).then_inc(total_ready, 1)
            dve.wait_ge(total_ready, r + 1)
            dve.reciprocal(rtotal[:, :], total[:, :]).then_inc(rtotal_ready, 1)

        def pool_scale(pool, r, s):
            pool.wait_ge(rtotal_ready, r + 1)
            pr = prob[:, s, :, :, 0:NTOK].rearrange("p a h m -> p (a h) m")
            pool.tensor_tensor(pr, pr, rtotal[:, :].unsqueeze(2).broadcast_to([128, PAIRS * HEADS, NTOK]),
                               ALU.mult).then_inc(prob_ready, 1)

        def pe_turn(pe, r, s, p):
            if p == 0:
                pe.wait_ge(prob_ready, r + 1)
            past(pe, pt_ready, 4 * r + max(p - 1, 0))
            for hp in range(3):
                mm = pe.transpose(PT[p % 2][:, hp * 128:(hp + 1) * 128],
                                  prob[:, s, p, 2 * hp:2 * hp + 2, :].rearrange("p h m -> p (h m)"),
                                  ident[:, :])
            mm.then_inc(pt_raw, 1)

        def pe_attend(pe, r, s, p):
            past(pe, pt_ready, 4 * r + p + 1)
            if p == 0:
                for half in range(2):
                    pe.wait_ge(v_ready[half], 4 * (r + 1))
            if p % 2 == 0:
                past(pe, o_ready, 2 * r + p // 2)
            for w in range(2):
                col = (2 * (p % 2) + w) * NTOK
                for hp in range(3):
                    rows = 64 * (hp % 2)
                    cols = col + (hp // 2) * (ROW // 2)
                    mm = pe.matmul(OB[rows:rows + 64, cols:cols + NTOK], vbd[:, s, 2 * p + w, hp, :],
                                   pt[:, p % 2, hp, 64 * w:64 * w + NTOK], start=True, stop=True)
            mm.then_inc(pv_done, 1)

        def act_turned(act, r, p):
            past(act, pt_raw, 4 * r + p + 1)
            past(act, pv_done, 4 * r + max(p - 1, 0))
            act.activation(pt[:, p % 2, :, :].rearrange("p h n -> p (h n)"), PT[p % 2][:, 0:384],
                           ACT.Copy).then_inc(pt_ready, 1)

        def act_outputs(act, r, s, half):
            past(act, pv_done, 4 * r + 2 * half + 2)
            lo, hi = half * (ROW // 2), (half + 1) * (ROW // 2)
            act.activation(o[:, s, 0, lo:hi], OB[:, 0:ROW // 2], ACT.Copy)
            act.activation(o[0:64, s, 1, lo:hi], OB[0:64, ROW // 2:ROW], ACT.Copy).then_inc(o_ready, 1)

        def pe_proj(pe, r, s, k_after):
            past(pe, o_ready, 2 * (r + 1))
            for c in range(NC):
                if k_after and c == 0:
                    pe.wait_ge(rest_ready, (1 + RH) * (r + 2))
                elif k_after:
                    pe.wait_ge(k_ready, r + 2)
                else:
                    past(pe, res_done[c], r)
                pe.matmul(QK[c][0:CH, 0:ROW], wp_sb[:, 0, c * CH:(c + 1) * CH], o[:, s, 0, :],
                          start=True, stop=False)
                pe.matmul(QK[c][0:CH, 0:ROW], wp_sb[0:64, 1, c * CH:(c + 1) * CH], o[0:64, s, 1, :],
                          start=False, stop=True).then_inc(proj_raw, 1)

        def dve_residual(dve, r):
            for c in range(NC):
                dve.wait_ge(proj_raw, 2 * r + c + 1)
                row = x[:, bass.ds(r % (2 * NWIN), 1), c, :].rearrange("p a n -> p (a n)")
                dve.scalar_tensor_tensor(out=row, in0=QK[c][0:CH, 0:ROW], scalar=bp[:, c:c + 1], in1=row,
                                         op0=ALU.add, op1=ALU.add).then_inc(res_done[c], 1)

        def dve_measure(dve, r, i, row):
            for c in range(NC):
                past(dve, res_done[c], r + 1)
            past(dve, summed_up, 3 * i)
            dve.sem_inc(stats.passed, 1)
            for c in range(NC):
                dve.bn_stats(bn1[:, c, bass.ds(row, 1), :].rearrange("p a n -> p (a n)"),
                             x[:, bass.ds(r % (2 * NWIN), 1), c, :].rearrange("p a n -> p (a n)")) \
                    .then_inc(measured, 1)

        def dve_sum_up(dve, i):
            dve.wait_ge(measured, 2 * NWIN * (i + 1))
            dve.sem_inc(stats.passed, 1)
            for c in range(NC):
                dve.bn_aggr(aggregate[:, c, :], bn1[:, c, :, :].rearrange("p a b -> p (a b)"))                     .then_inc(summed_up, 1)
            past(dve, summed_up, 3 * i + 2)
            dve.tensor_copy(mv1[:, bass.ds(i, 1), :, :].rearrange("p a c n -> p (a c n)"),
                            aggregate[:, :, :].rearrange("p c n -> p (c n)")).then_inc(summed_up, 1)


        def pe_step(pe, r, s, attend=True, front=True, statistics=None):
            if front:
                pe_qk(pe, r + 1, 1 - s)
            if statistics is not None:
                stats.mean_mm(pe, statistics)
            if front:
                pe_v(pe, r + 1, 1 - s, 0)
            if attend:
                pe_turn(pe, r, s, 0)
                pe_turn(pe, r, s, 1)
            if front:
                pe_logits(pe, r + 1, 1 - s, 0)
            if attend:
                if statistics is not None:
                    stats.var_mm(pe, statistics)
                    pe.wait_ge(stats.step, statistics * STAT_STEPS + 23)
                pe_attend(pe, r, s, 0)
                pe_turn(pe, r, s, 2)
                pe_attend(pe, r, s, 1)
                pe_turn(pe, r, s, 3)
            if front:
                pe_logits(pe, r + 1, 1 - s, 1)
            if attend:
                pe_attend(pe, r, s, 2)
                pe_attend(pe, r, s, 3)
            if front:
                pe_v(pe, r + 1, 1 - s, 1)
            if attend:
                pe_proj(pe, r, s, front)

        def dve_step(dve, r, s, attend=True, front=True, last_row=0, statistics=None, measure=None):
            if front:
                dve_k(dve, r + 1, 1 - s)
                if statistics is not None:
                    stats.spread(dve, statistics)
                dve_v(dve, r + 1, 1 - s)
                if statistics is not None:
                    stats.variance(dve, statistics)
                for half in range(2):
                    dve_bias(dve, r + 1, half, last_row)
                    dve_centre(dve, r + 1, half)
            if statistics is not None:
                stats.affine(dve, statistics)
            if measure is not None:
                image, row = measure
                dve.wait_ge(x_loaded, 16 * (image + 1))
                stats.rows(dve, image, (row, row + 1))
            if attend:
                dve_residual(dve, r)
            if front:
                dve_total(dve, r + 1, 1 - s)

        def act_step(act, r, s, attend=True, front=True, image=None, statistics=None):
            if front:
                act_q(act, r + 1, 1 - s)
            if attend:
                act_turned(act, r, 0)
                act_turned(act, r, 1)
                act_turned(act, r, 2)
                act_outputs(act, r, s, 0)
                act_turned(act, r, 3)
            if statistics is not None:
                stats.root(act, statistics)
            if attend:
                act_outputs(act, r, s, 1)
            if image is not None:
                act_norm(act, r + 2, image, s)
            if front:
                act_v(act, r + 1, 1 - s)
                act_exp(act, r + 1, 1 - s)

        block = ctx.enter_context(nc.Block())

        @block.sync
        def _(sp):
            for src, dst in ((w_qkv, wqkv[:, :, :]), (w_proj[0:128, :], wp_sb[:, 0, :]),
                             (w_proj[128:192, :], wp_sb[0:64, 1, :]),
                             (b_proj, bp[:, :]), (gmat_d, gmat[:, :]), (kmask_d, kmask[:, :]),
                             (ident_d, ident[:, :]), (rel, rel_sb[:, :, :]), (mask, mask_sb[:, :, :, :])):
                sp.dma_start(dst, src).then_inc(consts, 16)

            def load(i, slot):
                sp.dma_start(x[:, slot * NWIN:(slot + 1) * NWIN, :, :].rearrange("p a c n -> p (a c n)"),
                             x_in[bass.ds(i, 1), :, :].rearrange("a p n -> (a p) n")).then_inc(x_loaded, 16)

            def store(i, slot):
                for c in range(NC):
                    past(sp, res_done[c], NWIN * (i + 1))
                sp.dma_start(x1[bass.ds(i, 1), :, :].rearrange("a p n -> (a p) n"),
                             x[:, slot * NWIN:(slot + 1) * NWIN, :, :].rearrange("p a c n -> p (a c n)")) \
                    .then_inc(x_stored, 16)
                sp.wait_ge(x_stored, 16 * (i + 1))

            load(0, 0)
            sp.wait_ge(x_loaded, 16)
            load(1, 1)
            with sp.Fori(0, B // 2 - 1) as pair:
                for slot in range(2):
                    store(2 * pair + slot, slot)
                    sp.wait_ge(x_loaded, 16 * (2 * pair + slot + 2))
                    sp.wait_ge(measured, 2 * NWIN * (2 * pair + slot + 1))
                    load(2 * pair + slot + 2, slot)
            for slot in range(2):
                store(B - 2 + slot, slot)

        @block.gpsimd
        def _(pool):
            start_at_one(pool, *res_done, summed_up, s_raw, pv_done, pt_raw, pt_ready, o_ready)
            for t in (xn[:, :, :, :, NTOK:PADW], q[:, :, :, NTOK:PADW], q_rest[:, :, :, NTOK:PADW],
                      kbd_rest[:, :, :, :], prob[:, :, :, :, NTOK:PADW], vbd[:, :, :, :, :]):
                pool.memset(t, 0.0).then_inc(zeroed, 1)
            pool.wait_ge(zeroed, ZEROED - 1)
            pool.memset(xn[CH:CH + 1, :, 1, :, 0:NTOK], 1.0).then_inc(zeroed, 1)
            pool_scale(pool, 0, 0)

            def image(i, last):
                with pool.Fori(0, 3) as p:
                    pool_scale(pool, i * NWIN + 2 * p + 1, 1)
                    pool_scale(pool, i * NWIN + 2 * p + 2, 0)
                pool_scale(pool, i * NWIN + 7, 1)
                if not last:
                    pool_scale(pool, i * NWIN + 8, 0)

            with pool.Fori(0, B - 1) as i:
                image(i, False)
            image(B - 1, True)

        @block.vector
        def _(dve):
            dve.wait_ge(consts, 16 * NCONST)
            for last_row in range(2):
                for p in range(PAIRS):
                    dve.tensor_tensor(bias[:, last_row, p, :, :], rel_sb[:, :, :],
                                      mask_sb[:, last_row, p, :].unsqueeze(1)
                                      .broadcast_to([128, HEADS, NTOK]), ALU.add).then_inc(bias_ready, 1)
            dve.wait_ge(bias_ready, 2 * PAIRS)
            dve.wait_ge(zeroed, ZEROED)
            dve.wait_ge(x_loaded, 16)
            stats.rows(dve, 0, range(NWIN))
            stats.aggregate(dve, 0)
            stats.spread(dve, 0)
            stats.variance(dve, 0)
            stats.affine(dve, 0)
            dve_step(dve, -1, 1, attend=False)

            def image(i, last):
                def pair(j0, step_rows=0, last_pair=False):
                    for k in range(2):
                        dve_step(dve, i * NWIN + j0 + k, k, front=not (last and last_pair and k == 1),
                                 last_row=int(last_pair and k == 0),
                                 statistics=i + 1 if last_pair and k == 0 and not last else None,
                                 measure=(i + 1, step_rows + 2 * k)
                                 if step_rows is not None and not last else None)
                        dve_measure(dve, i * NWIN + j0 + k, i, j0 + k)

                pair(0, None)
                with dve.Fori(1, 3) as p:
                    pair(2 * p, 4 * p - 4)
                if not last:
                    stats.aggregate(dve, i + 1)
                pair(6, None, True)
                dve_sum_up(dve, i)

            with dve.Fori(0, B - 1) as i:
                image(i, False)
            image(B - 1, True)

        @block.scalar
        def _(act):
            act.wait_ge(zeroed, ZEROED)
            act.wait_ge(x_loaded, 16)
            stats.root(act, 0)
            act_norm(act, 0, 0, 0)
            act_step(act, -1, 1, attend=False, image=0)

            def image(i, last):
                def pair(j0, last_pair=False):
                    for k in range(2):
                        end = last and last_pair
                        act_step(act, i * NWIN + j0 + k, k, front=not (end and k == 1),
                                 image=None if end else i + 1 if last_pair else i,
                                 statistics=i + 1 if last_pair and k == 0 and not last else None)

                with act.Fori(0, 3) as p:
                    pair(2 * p)
                if not last:
                    act.wait_ge(x_loaded, 16 * (i + 2))
                pair(6, True)

            with act.Fori(0, B - 1) as i:
                image(i, False)
            image(B - 1, True)

        @block.tensor
        def _(pe):
            pe.wait_ge(consts, 16 * NCONST)
            pe.wait_ge(zeroed, ZEROED)
            stats.mean_mm(pe, 0)
            stats.var_mm(pe, 0)
            pe_step(pe, -1, 1, attend=False)

            def image(i, last):
                def pair(j0, last_pair=False):
                    for k in range(2):
                        pe_step(pe, i * NWIN + j0 + k, k, front=not (last and last_pair and k == 1),
                                statistics=i + 1 if last_pair and k == 0 and not last else None)

                with pe.Fori(0, 3) as p:
                    pair(2 * p)
                pair(6, True)

            with pe.Fori(0, B - 1) as i:
                image(i, False)
            image(B - 1, True)


def outlook_layer(nc, x1, mv, out, w_v, w_a, b_a, w_proj, b_proj, gmat_d):
    with ExitStack() as ctx:
        def sb(name, shape):
            return ctx.enter_context(nc.sbuf_tensor(name, shape, F32))

        def sem(name):
            return ctx.enter_context(nc.semaphore(name))

        bank = [ctx.enter_context(nc.psum_tensor(f"l1_bank{i}", [128, 512], F32)) for i in range(8)]
        OB, VB = bank[0:6], bank[6:8]
        IB = 5
        bank_rows = [range(i, min(i + IB, HN)) for i in range(0, HN, IB)]
        NB = len(bank_rows)
        NG = NC * 2
        NH = NG * HC
        PP = KK * KK
        JP = HALF // 2
        PARTS = [range(0, 8), range(8, HALF)]
        SLOTS = 4
        TSLOTS = HC
        ZSLOTS = 2
        ops = NWIN // SLOTS

        rows = sb("rows", [CH, SLOTS, NC, ROW])
        wv = sb("wv", [CH, NC, C])
        wa = sb("wa", [CH, NC, 2 * AH])
        ba = sb("ba", [128, AH])
        wp_sb = sb("wp1", [CH, NC, C])
        bp = sb("bp1", [CH, NC])
        gmat = sb("gmat1", [CH, CH])
        norm = sb("norm1", [CH, 2, B, NC])
        xn = sb("xn1", [CH, 2, NC, 2, RAS, SX])
        y = sb("y", [CH, NC, RAS, RAS])
        rowsum = sb("rowsum", [CH, HALF, 2 * HALF])
        pooled = sb("pooled", [CH, NC, HALF, 2, IP])
        a = sb("a", [128, HALF, AH])
        total = sb("total1", [128, HALF, HC * KK])
        z = sb("z", [CH, ZSLOTS, TC * SX])
        t = sb("t", [CH, TSLOTS, TC * IP])
        v = sb("v", [CH, HN, CH])
        o = sb("o1", [CH, HN, TC])

        consts, zeroed, passed = sem("consts1"), sem("zeroed1"), sem("passed1")
        normed = sem("normed")
        x_loaded = [sem(f"x_loaded{s}") for s in range(SLOTS)]
        res_loaded = [sem(f"res_loaded{s}") for s in range(SLOTS)]
        out_stored = [sem(f"out_stored{s}") for s in range(SLOTS)]
        xn_raw, xn_act, xn_ready = sem("xn1_raw"), sem("xn1_act"), sem("xn1_ready")
        rowsum_ready, pooled_ready = sem("rowsum_ready"), sem("pooled_ready")
        a_raw, a_biased = sem("a_raw"), sem("a_biased")
        top_ready, a_centred, a_exp = sem("top1_ready"), sem("a_centred"), sem("a_exp")
        total_ready, rtotal_ready = sem("total1_ready"), sem("rtotal1_ready")
        a_scaled, a_ready = sem("a_scaled"), sem("a_ready")
        z_begun, z_ready, t_ready = sem("z_begun"), sem("z_ready"), sem("t_ready")
        v_raw, v_ready = sem("v1_raw"), sem("v1_ready")
        o_raw, o_ready = sem("o1_raw"), sem("o1_ready")
        folded, y_ready = sem("folded"), sem("y_ready")
        proj_raw = sem("proj1_raw")
        res_done = [sem(f"res1_done{p}") for p in range(3)]
        PAIR_ROWS = [len(range(p, NWIN, 3)) for p in range(3)]
        NORMS = 2 * NC
        ACT_ROW = 2
        POOLS = NC * 2 * 2
        FOLDED = [0, 3, 8, 11]
        ZEROED = 7
        FOLDS = 16


        STATS_PSUM = VB[0][0:CH, 0:B * NC]

        def flat(s):
            return s.rearrange("p i c -> p (i c)")

        def pe_norms(pe):
            pe.matmul(STATS_PSUM, gmat[:, :], flat(mv[:, :, :, 0]), start=True, stop=True).then_inc(normed, 1)
            pe.wait_ge(normed, 5)
            pe.matmul(STATS_PSUM, gmat[:, :], flat(mv[:, :, :, 0]), start=True, stop=True).then_inc(normed, 1)
            pe.wait_ge(normed, 7)

        def dve_norms(dve):
            dve.wait_ge(normed, 1)
            dve.tensor_tensor(flat(mv[:, :, :, 0]), flat(mv[:, :, :, 0]), STATS_PSUM, ALU.subtract) \
                .then_inc(normed, 1)
            dve.tensor_copy(flat(norm[:, 1, :, :]), STATS_PSUM).then_inc(normed, 1)
            dve.wait_ge(normed, 3)
            dve.tensor_tensor(flat(mv[:, :, :, 0]), flat(mv[:, :, :, 0]), flat(mv[:, :, :, 0]), ALU.mult) \
                .then_inc(normed, 1)
            dve.wait_ge(normed, 4)
            dve.tensor_tensor(flat(mv[:, :, :, 0]), flat(mv[:, :, :, 0]), flat(mv[:, :, :, 1]), ALU.add) \
                .then_inc(normed, 1)
            dve.wait_ge(normed, 6)
            dve.tensor_scalar(flat(mv[:, :, :, 0]), STATS_PSUM, GN_EPS, None, ALU.add).then_inc(normed, 1)
            scale, bias = flat(norm[:, 0, :, :]), flat(norm[:, 1, :, :])
            dve.wait_ge(normed, 8)
            dve.reciprocal(scale, flat(mv[:, :, :, 0])).then_inc(normed, 1)
            dve.wait_ge(normed, 9)
            dve.scalar_tensor_tensor(out=bias, in0=bias, scalar=-1.0, in1=scale,
                                     op0=ALU.mult, op1=ALU.mult).then_inc(normed, 1)
            dve.wait_ge(normed, 10)

        def act_norms(act):
            act.wait_ge(normed, 7)
            act.activation(flat(mv[:, :, :, 0]), flat(mv[:, :, :, 0]), ACT.Sqrt).then_inc(normed, 1)
            act.wait_ge(normed, 10)


        def norm_pieces(i, s, row):
            first = WIN * row + SHIFT + 1
            return [(xn[:, s, c, f, first:first + WIN, SHIFT + 1:SX].rearrange("p r (w n) -> p w r n", n=WIN),
                     rows[:, row % SLOTS, c, f * ROW // 2:(f + 1) * ROW // 2]
                     .rearrange("p (w r n) -> p w r n", r=WIN, n=WIN),
                     norm[:, 0, bass.ds(i, 1), c], norm[:, 1, bass.ds(i, 1), c])
                    for c in range(NC) for f in range(2)]

        def dve_norm(dve, i, s, row):
            dve.wait_ge(x_loaded[row % SLOTS], 16 * (ops * i + row // SLOTS + 1))
            if row == 0:
                past(dve, v_raw, NG * NB * (i - 1))
            dve.sem_inc(passed, 1)
            for raster, x, scale, shift in norm_pieces(i, s, row):
                dve.tensor_scalar(raster, x, scale, shift, ALU.mult, ALU.add).then_inc(xn_raw, 1)

        def act_norm(act, i, s):
            act.wait_ge(x_loaded[ACT_ROW], 16 * (ops * i + 1))
            past(act, v_raw, NG * NB * (i - 1))
            act.sem_inc(passed, 1)
            for raster, x, scale, shift in norm_pieces(i, s, ACT_ROW):
                act.activation(raster, x, ACT.Identity, bias=shift, scale=scale).then_inc(xn_act, 1)

        def rows_normed(i, row):
            return NORMS * ((NWIN - 1) * i + row + 1 - (row >= ACT_ROW))

        def pool_wrap_xn(pool, i, s):
            pool.wait_ge(xn_raw, rows_normed(i, NWIN - 1))
            pool.wait_ge(xn_act, NORMS * (i + 1))
            pool.sem_inc(passed, 1)
            for c in range(NC):
                pool.tensor_copy(xn[:, s, c, 0, SHIFT + 1:RAS, 1:SHIFT + 1],
                                 xn[:, s, c, 1, SHIFT + 1:RAS, SX - SHIFT:SX]).then_inc(xn_ready, 1)
                pool.tensor_copy(xn[:, s, c, 1, SHIFT + 1:RAS, 0:SHIFT + 1],
                                 xn[:, s, c, 0, SHIFT + 1:RAS, 2 * HALF:SX]).then_inc(xn_ready, 1)
            pool.wait_ge(xn_ready, 6 * i + 4)
            pool.sem_inc(passed, 1)
            for c in range(NC):
                pool.tensor_copy(xn[:, s, c, :, 1:SHIFT + 1, :], xn[:, s, c, :, H + 1:RAS, :]) \
                    .then_inc(xn_ready, 1)

        def dve_pool(dve, i, s, c):
            dve.wait_ge(xn_ready, 6 * (i + 1))
            for n in range(4 * c, 4 * c + 4):
                f, i0 = n // 2 % 2, HALF * (n % 2)
                at(dve, pooled_ready, POOLS * i + n)
                r0, r1 = 1 + 2 * i0, 1 + 2 * (i0 + HALF)
                dve.tensor_tensor(rowsum[:, :, :], xn[:, s, c, f, r0:r1:2, 1:2 * HALF + 1],
                                  xn[:, s, c, f, r0 + 1:r1 + 1:2, 1:2 * HALF + 1], ALU.add) \
                    .then_inc(rowsum_ready, 1)
                dve.wait_ge(rowsum_ready, POOLS * i + n + 1)
                pair = rowsum[:, :, :].rearrange("p i (j b) -> p i j b", b=2)
                dve.tensor_tensor(pooled[:, c, :, f, i0:i0 + HALF].rearrange("p j i -> p i j"),
                                  pair[:, :, :, 0], pair[:, :, :, 1], ALU.add).then_inc(pooled_ready, 1)

        def pe_logits(pe, i):
            pe.wait_ge(pooled_ready, POOLS * (i + 1))
            for jp in range(JP):
                if jp < 2:
                    at(pe, v_ready, NG * NB * i)
                else:
                    pe.wait_ge(a_biased, JP * i + jp - 1)
                for j in range(2):
                    for kc in range(NC):
                        for hc in range(NC):
                            mm = pe.matmul(VB[(jp + 1) % 2][64 * hc:64 * hc + 64, j * AH:(j + 1) * AH],
                                           pooled[:, kc, 2 * jp + j, :, :].rearrange("p f i -> p (f i)"),
                                           wa[:, kc, hc * AH:(hc + 1) * AH], start=(kc == 0), stop=(kc == NC - 1))
                mm.then_inc(a_raw, 1)

        def part(n):
            return a[:, PARTS[n].start:PARTS[n].stop, :].rearrange("P j (x q) -> P (j x) q", q=KK)

        def of_part(n):
            return total[:, PARTS[n].start:PARTS[n].stop, :].rearrange("P j x -> P (j x)")

        def dve_logits(dve, i, jp):
            if jp == 0:
                at(dve, z_ready, K * NH * i)
            dve.wait_ge(a_raw, JP * i + jp + 1)
            dve.scalar_tensor_tensor(out=a[:, 2 * jp:2 * jp + 2, :],
                                     in0=VB[(jp + 1) % 2][:, 0:2 * AH].rearrange("p (j a) -> p j a", j=2),
                                     scalar=0.25, in1=ba[:, :].unsqueeze(1).broadcast_to([128, 2, AH]),
                                     op0=ALU.mult, op1=ALU.add).then_inc(a_biased, 1)

        def dve_top(dve, i, n):
            dve.wait_ge(a_biased, JP * i + PARTS[n].stop // 2)
            at(dve, a_scaled, HC * i)
            dve.tensor_reduce(of_part(n), part(n), AX.X, ALU.max).then_inc(top_ready, 1)

        def dve_centre(dve, i, n):
            dve.wait_ge(top_ready, 2 * i + n + 1)
            top = of_part(n).unsqueeze(2).broadcast_to([128, len(PARTS[n]) * HC * KK, KK])
            dve.tensor_tensor(part(n), part(n), top, ALU.subtract).then_inc(a_centred, 1)

        def act_exp(act, i, n):
            act.wait_ge(a_centred, 2 * i + n + 1)
            act.activation(part(n), part(n), ACT.Exp, scale=QSCALE).then_inc(a_exp, 1)

        def dve_total(dve, i, n):
            dve.wait_ge(a_exp, 2 * i + n + 1)
            dve.tensor_reduce(of_part(n), part(n), AX.X, ALU.add).then_inc(total_ready, 1)
            dve.wait_ge(total_ready, 2 * i + n + 1)
            dve.reciprocal(of_part(n), of_part(n)).then_inc(rtotal_ready, 1)

        def dve_softmax(dve, i):
            for jp in range(JP):
                dve_logits(dve, i, jp)
                if jp == 3:
                    dve_top(dve, i, 0)
                if jp == 5:
                    dve_centre(dve, i, 0)
            dve_top(dve, i, 1)
            dve_centre(dve, i, 1)
            dve_total(dve, i, 0)
            dve_total(dve, i, 1)

        def pool_scale(pool, i, h):
            pool.wait_ge(rtotal_ready, 2 * (i + 1))
            head = a[:, :, h * PP:(h + 1) * PP].rearrange("P j (p q) -> P j p q", q=KK)
            pool.tensor_tensor(head, head, total[:, :, h * KK:(h + 1) * KK].unsqueeze(3)
                               .broadcast_to([128, HALF, KK, KK]), ALU.mult).then_inc(a_scaled, 1)
            first = h * PP
            left = a[:, 0:HALF - 1, first + 2 * K * KK + K - 1:first + KK * KK:K]
            right = a[:, 1:HALF, first:first + K * KK:K]
            pool.wait_ge(a_scaled, HC * i + h + 1)
            pool.tensor_tensor(left, left, right, ALU.add).then_inc(a_ready, 1)

        def act_spread(act, i, hs):
            g, h = hs // HC, hs % HC
            act.wait_ge(a_ready, HC * i + h + 1)
            at(act, t_ready, NH * i + hs + 1 - ZSLOTS)
            for p0, p1 in ((0, 2 * K), (2 * K, KK)):
                if p0:
                    act.wait_ge(z_begun, K * (NH * i + hs + 1))
                for qy in range(K):
                    first = z[32 * qy:32 * qy + 32, hs % ZSLOTS, p0 * SX:p0 * SX + 1]
                    diagonal = bass.AP(first.tensor, first.offset,
                                       [[first.ap[0][0], 32], [SX, p1 - p0], [2 * K * SX + 2, HALF], [1, K]])
                    src = a[32 * g:32 * g + 32, :, h * PP:(h + 1) * PP].rearrange(
                        "P j (p u v) -> P u p j v", u=K, v=K)[:, qy, p0:p1, :, :]
                    act.activation(diagonal, src, ACT.Copy).then_inc(z_ready if p0 else z_begun, 1)

        def dve_turn(dve, i, hs):
            dve.wait_ge(z_ready, K * (NH * i + hs + 1))
            past(dve, o_raw, NB * (NG * i + hs // HC))
            dve.transpose(t[:, hs % TSLOTS, :], z[:, hs % ZSLOTS, :]).then_inc(t_ready, 1)

        def pe_values(pe, i, g, s):
            c, f = g // 2, g % 2
            for kb in range(NB):
                if g == 0 and kb < 2:
                    pe.wait_ge(a_biased, JP * (i + 1) - 1 + kb)
                at(pe, v_ready, NB * (NG * i + g) + kb - 1)
                for k, row in enumerate(bank_rows[kb]):
                    for kc in range(NC):
                        mm = pe.matmul(VB[kb % 2][0:CH, k * CH:(k + 1) * CH],
                                       xn[:, s, kc, f, 2 * row:2 * row + K, :].rearrange("p r x -> p (r x)"),
                                       wv[:, kc, c * CH:(c + 1) * CH], start=(kc == 0), stop=(kc == NC - 1))
                mm.then_inc(v_raw, 1)

        def act_values(act, i, g, kb):
            past(act, v_raw, NB * (NG * i + g) + kb + 1)
            r = bank_rows[kb]
            act.activation(v[:, r.start:r.stop, :].rearrange("p i d -> p (i d)"),
                           VB[kb % 2][0:CH, 0:len(r) * CH], ACT.Copy).then_inc(v_ready, 1)

        def pe_heads(pe, i, g):
            pe.wait_ge(t_ready, NH * i + HC * (g + 1))
            for kb in range(NB):
                if g == 0 and kb % 2 == 0:
                    past(pe, res_done[kb // 2], 2 * PAIR_ROWS[kb // 2] * i)
                pe.wait_ge(v_ready, NB * (NG * i + g) + kb + 1)
                if g > 0:
                    pe.wait_ge(o_ready, NB * (NG * i + g - 1) + kb + 1)
                for k, row in enumerate(bank_rows[kb]):
                    for h in range(HC):
                        turned = t[:, (HC * g + h) % TSLOTS, :].rearrange("p (n i) -> p n i", i=IP)
                        mm = pe.matmul(OB[kb][32 * h:32 * h + 32, k * TC:(k + 1) * TC],
                                       v[:, row, HD * h:HD * (h + 1)], turned[:, :, row],
                                       start=True, stop=True)
                mm.then_inc(o_raw, 1)

        def act_outputs(act, i, g, kb):
            past(act, o_raw, NB * (NG * i + g) + kb + 1)
            past(act, folded, FOLDS * i + FOLDED[g])
            r = bank_rows[kb]
            act.activation(o[:, r.start:r.stop, :].rearrange("p i n -> p (i n)"),
                           OB[kb][0:CH, 0:len(r) * TC], ACT.Copy).then_inc(o_ready, 1)

        def pool_fold(pool, i, g):
            c, f = g // 2, g % 2
            pool.wait_ge(o_ready, NB * (NG * i + g + 1))
            if g == 0:
                past(pool, proj_raw, 2 * NWIN * i)
            pool.sem_inc(passed, 1)
            out = o[:, :, :].rearrange("p i (x r) -> p i x r", r=K)
            steps = [(1, 1, XT, False), (2, 1, XT, False)]
            if f == 1:
                steps += [(1, 0, 1, True), (2, 0, 1, True)]
            steps += [(0, 1 - f, XT, True)]
            for n, (py, x0, x1_, add) in enumerate(steps):
                i0 = 1 if py == 0 else 0
                r0 = 2 * i0 + py
                dst = y[:, c, r0:r0 + 2 * (HN - i0) - 1:2, 2 * HALF * f + x0:2 * HALF * f + x1_]
                src = out[:, i0:HN, x0:x1_, py]
                if add:
                    past(pool, folded, FOLDS * i + FOLDED[g] + n)
                    pool.tensor_tensor(dst, dst, src, ALU.add).then_inc(folded, 1)
                else:
                    pool.tensor_copy(dst, src).then_inc(folded, 1)

        def pool_wrap_y(pool, i):
            past(pool, folded, FOLDS * (i + 1))
            pool.sem_inc(passed, 1)
            for c in range(NC):
                pool.tensor_copy(y[:, c, 1:H + 1, W + 1:RAS], y[:, c, 1:H + 1, 1:SHIFT + 1]).then_inc(y_ready, 1)
            pool.wait_ge(y_ready, 4 * i + 2)
            pool.sem_inc(passed, 1)
            for c in range(NC):
                pool.tensor_copy(y[:, c, H + 1:RAS, 1:RAS], y[:, c, 1:SHIFT + 1, 1:RAS]).then_inc(y_ready, 1)

        def proj_bank(row, c):
            return OB[2 * (row % 3) + c][0:CH, 0:ROW]

        def pe_proj(pe, i):
            pe.wait_ge(y_ready, 4 * (i + 1))
            for row in range(NWIN):
                if row >= 3:
                    past(pe, res_done[row % 3], 2 * (PAIR_ROWS[row % 3] * i + row // 3))
                first = WIN * row + SHIFT + 1
                for c in range(NC):
                    for kc in range(NC):
                        mm = pe.matmul(proj_bank(row, c), wp_sb[:, kc, c * CH:(c + 1) * CH],
                                       y[:, kc, first:first + WIN, SHIFT + 1:RAS]
                                       .rearrange("p r (w n) -> p w r n", n=WIN),
                                       start=(kc == 0), stop=(kc == NC - 1))
                    mm.then_inc(proj_raw, 1)

        def dve_residual(dve, i, row):
            dve.wait_ge(res_loaded[row % SLOTS], 16 * (ops * i + row // SLOTS + 1))
            for c in range(NC):
                past(dve, proj_raw, 2 * (NWIN * i + row) + c + 1)
                r = rows[:, row % SLOTS, c, :]
                dve.scalar_tensor_tensor(out=r, in0=proj_bank(row, c), scalar=bp[:, c:c + 1], in1=r,
                                         op0=ALU.add, op1=ALU.add).then_inc(res_done[row % 3], 1)

        block = ctx.enter_context(nc.Block())

        def images(engine, image):
            with engine.Fori(0, B // 2 - 1) as pair:
                for s in range(2):
                    image(2 * pair + s, s, False)
            image(B - 2, 0, False)
            image(B - 1, 1, True)

        @block.sync
        def _(sp):
            for src, dst in ((w_v, wv[:, :, :]), (w_a, wa[:, :, :]), (w_proj, wp_sb[:, :, :]),
                             (b_proj, bp[:, :]), (gmat_d, gmat[:, :]),
                             (b_a[0:1, :].broadcast_to([64, AH]), ba[0:64, :]),
                             (b_a[1:2, :].broadcast_to([64, AH]), ba[64:128, :])):
                sp.dma_start(dst, src).then_inc(consts, 16)

            def dram_row(dram, i, row):
                return dram[bass.ds(i, 1), :, NC * ROW * row:NC * ROW * (row + 1)].rearrange("a p n -> (a p) n")

            def ring(row):
                return rows[:, row % SLOTS, :, :].rearrange("p c n -> p (c n)")

            def load_for_norm(i):
                for row in range(NWIN):
                    if row < SLOTS:
                        past(sp, out_stored[row], 16 * ops * (i - 1))
                    elif row - SLOTS == ACT_ROW:
                        sp.wait_ge(xn_act, NORMS * (i + 1))
                    else:
                        sp.wait_ge(xn_raw, rows_normed(i, row - SLOTS))
                    sp.dma_start(ring(row), dram_row(x1, i, row)).then_inc(x_loaded[row % SLOTS], 16)

            def load_for_residual(i, row):
                sp.dma_start(ring(row), dram_row(x1, i, row)).then_inc(res_loaded[row % SLOTS], 16)

            def wait_stored(i, row):
                past(sp, out_stored[row % SLOTS], 16 * (ops * i + row // SLOTS + 1))

            def image(i, s, last):
                if not last:
                    load_for_norm(i + 1)
                for row in range(SLOTS):
                    if last:
                        past(sp, out_stored[row], 16 * ops * i)
                    else:
                        sp.wait_ge(xn_raw, rows_normed(i + 1, SLOTS + row))
                    load_for_residual(i, row)
                for row in range(NWIN):
                    past(sp, res_done[row % 3], 2 * (PAIR_ROWS[row % 3] * i + row // 3 + 1))
                    sp.dma_start(dram_row(out, i, row), ring(row)).then_inc(out_stored[row % SLOTS], 16)
                    if 1 <= row <= SLOTS:
                        wait_stored(i, row - 1)
                        load_for_residual(i, row - 1 + SLOTS)
                if last:
                    for row in range(SLOTS, NWIN):
                        wait_stored(i, row)

            load_for_norm(0)
            sp.wait_ge(xn_raw, rows_normed(0, NWIN - 1))
            images(sp, image)

        @block.gpsimd
        def _(pool):
            start_at_one(pool, o_raw, v_raw, folded, proj_raw, *res_done, *out_stored)
            for s in range(2):
                pool.memset(xn[:, s, :, :, 0, :], 0.0).then_inc(zeroed, 1)
            pool.memset(pooled[:, :, :, :, HN:IP], 0.0).then_inc(zeroed, 1)
            pool.memset(z[:, 0, :], 0.0).then_inc(zeroed, 1)
            for s in range(2):
                pool.memset(xn[:, s, :, 0, 1:RAS, 0], 0.0).then_inc(zeroed, 1)
            pool_wrap_xn(pool, 0, 0)
            for h in range(HC):
                pool_scale(pool, 0, h)

            def image(i, s, last):
                for g in range(NG):
                    if g == 1 and not last:
                        pool_wrap_xn(pool, i + 1, 1 - s)
                    pool_fold(pool, i, g)
                pool_wrap_y(pool, i)
                if not last:
                    for h in range(HC):
                        pool_scale(pool, i + 1, h)

            images(pool, image)

        @block.vector
        def _(dve):
            dve.memset(z[:, 1, :], 0.0).then_inc(zeroed, 1)
            dve.wait_ge(consts, 16 * 7)
            dve.wait_ge(zeroed, ZEROED)
            dve_norms(dve)
            for row in range(NWIN):
                if row != ACT_ROW:
                    dve_norm(dve, 0, 0, row)
            for c in range(NC):
                dve_pool(dve, 0, 0, c)
            dve_softmax(dve, 0)
            for hs in range(HC):
                dve_turn(dve, 0, hs)

            def image(i, s, last):
                for g in range(NG):
                    if not last and g < 2:
                        for row in (range(0, ACT_ROW), range(ACT_ROW + 1, NWIN))[g]:
                            dve_norm(dve, i + 1, 1 - s, row)
                    if not last and g >= 2:
                        dve_pool(dve, i + 1, 1 - s, g - 2)
                    if g < NG - 1:
                        for h in range(HC):
                            dve_turn(dve, i, HC * (g + 1) + h)
                if not last:
                    dve_softmax(dve, i + 1)
                for row in range(NWIN):
                    dve_residual(dve, i, row)
                    if not last and row in (1, 3, 5):
                        dve_turn(dve, i + 1, row // 2)

            images(dve, image)

        @block.scalar
        def _(act):
            act.wait_ge(zeroed, ZEROED)
            act_norms(act)
            act_norm(act, 0, 0)

            def begin(i):
                act_exp(act, i, 0)
                act_values(act, i, 0, 0)
                act_values(act, i, 0, 1)
                act_exp(act, i, 1)
                for kb in range(2, NB):
                    act_values(act, i, 0, kb)
                act_spread(act, i, 0)
                act_spread(act, i, 1)
                act_spread(act, i, 2)

            begin(0)

            def image(i, s, last):
                act_spread(act, i, HC)
                for g in range(NG):
                    more = g < NG - 1
                    nxt = HC * (g + 1)
                    if more:
                        act_spread(act, i, nxt + 1)
                    for kb in range(NB):
                        act_outputs(act, i, g, kb)
                    if g == 0 and not last:
                        act_norm(act, i + 1, 1 - s)
                    if more:
                        for kb in range(NB):
                            act_values(act, i, g + 1, kb)
                            if kb == 1:
                                act_spread(act, i, nxt + 2)
                            if kb == 3 and g < NG - 2:
                                act_spread(act, i, nxt + HC)
                if not last:
                    begin(i + 1)

            images(act, image)

        @block.tensor
        def _(pe):
            pe.wait_ge(consts, 16 * 7)
            pe.wait_ge(zeroed, ZEROED)
            pe_norms(pe)
            pe_logits(pe, 0)
            pe_values(pe, 0, 0, 0)

            def image(i, s, last):
                for g in range(NG):
                    pe_heads(pe, i, g)
                    if g < NG - 1:
                        pe_values(pe, i, g + 1, s)
                if not last:
                    pe_logits(pe, i + 1)
                    pe_values(pe, i + 1, 0, 1 - s)
                pe_proj(pe, i)

            images(pe, image)


def preact_block(nc, x, w_qkv, w_proj, b_proj, rel, mask, gmat, kmask, ident, w_v, w_a, b_a,
                 w_proj1, b_proj1, out):
    x1 = nc.dram_tensor("x1_scratch", [B, CH, NWIN * NC * ROW], F32, kind="Internal").ap()
    with nc.sbuf_tensor("mv1", [CH, B, NC, 2], F32) as mv1:
        window_layer(nc, x, x1, mv1, w_qkv, w_proj, b_proj, rel, mask, gmat, kmask, ident)
        outlook_layer(nc, x1, mv1, out, w_v, w_a, b_a, w_proj1, b_proj1, gmat)



def shift_mask():
    region = np.zeros((H, W), np.float32)
    cuts = ((0, H - WIN), (H - WIN, H - SHIFT), (H - SHIFT, H))
    for n, (h0, h1) in enumerate(cuts):
        for m, (w0, w1) in enumerate(cuts):
            region[h0:h1, w0:w1] = 3 * n + m
    win = region.reshape(NWIN, WIN, NWIN, WIN).transpose(0, 2, 1, 3).reshape(NWIN, NWIN, NTOK)
    out = np.zeros((2, PADW, 2, PAIRS, NTOK), np.float32)
    for last_row, wy in enumerate((0, NWIN - 1)):
        for wx in range(NWIN):
            differ = win[wy, wx][:, None] != win[wy, wx][None, :]
            out[wx % 2, :NTOK, last_row, wx // 2] = np.where(differ, np.float32(-100), np.float32(0))
    return out.reshape(128, 2, PAIRS, NTOK)


def rel_index():
    coords = np.stack(np.meshgrid(np.arange(WIN), np.arange(WIN), indexing="ij")).reshape(2, -1)
    rel = coords[:, :, None] - coords[:, None, :] + WIN - 1
    return rel[0] * (2 * WIN - 1) + rel[1]


def column_first(w):
    w = w.reshape(-1, HEADS, K, K, KK).transpose(0, 1, 3, 2, 4)
    return np.ascontiguousarray(w.reshape(-1, HEADS * KK * KK))



def to_windows(x):
    x = np.roll(x, (-SHIFT, -SHIFT), axis=(1, 2))
    x = x.reshape(B, NWIN, WIN, NWIN, WIN, NC, CH).transpose(0, 6, 1, 5, 3, 2, 4)
    return np.ascontiguousarray(x.reshape(B, CH, NWIN * NC * ROW))


def from_windows(x):
    x = x.reshape(B, CH, NWIN, NC, NWIN, WIN, WIN).transpose(0, 2, 5, 4, 6, 3, 1)
    return np.ascontiguousarray(np.roll(x.reshape(B, H, W, C), (SHIFT, SHIFT), axis=(1, 2)))


def kernel(**inputs):
    import concourse.bacc as _bacc
    from concourse.bass_utils import run_bass_kernel_spmd as _run

    a = {k: np.asarray(v) for k, v in inputs.items()}

    def chunked(w):
        return np.ascontiguousarray(w.reshape(NC, CH, -1).transpose(1, 0, 2))

    order = np.r_[0:128, C:C + 128, 128:C, C + 128:2 * C, 2 * C:3 * C]
    w_qkv = np.zeros((CH + 1, NC, 3 * C), np.float32)
    w_qkv[:CH] = chunked(a["L0_conv_qkv_weight"][order].T)
    w_qkv[CH, 1] = a["L0_conv_qkv_bias"][order]
    rel = np.zeros((2, PADW, HEADS, NTOK), np.float32)
    rel[:, :NTOK] = a["L0_conv_rel_bias_table"][rel_index()].transpose(0, 2, 1)[None]
    arrays = {
        "x": to_windows(a["x"]),
        "w_qkv": w_qkv,
        "w_proj": np.ascontiguousarray(a["L0_conv_proj_weight"].T),
        "b_proj": np.ascontiguousarray(a["L0_conv_proj_bias"].reshape(NC, CH).T),
        "rel": rel.reshape(128, HEADS, NTOK),
        "mask": shift_mask(),
        "gmat": np.kron(np.eye(CH // GC), np.full((GC, GC), 1.0 / GC)).astype(np.float32),
        "kmask": np.kron(np.eye(QH), np.ones((HD, 1))).astype(np.float32),
        "ident": np.eye(128, dtype=np.float32),
        "w_v": chunked(a["L1_conv_Wv"]),
        "w_a": chunked(column_first(a["L1_conv_Wa"])),
        "b_a": column_first(a["L1_conv_ba"]).reshape(NC, AH),
        "w_proj1": chunked(a["L1_conv_Wp"]),
        "b_proj1": np.ascontiguousarray(a["L1_conv_bp"].reshape(NC, CH).T),
    }
    nc = _bacc.Bacc("TRN2", target_bir_lowering=False, num_devices=1)
    aps = [nc.dram_tensor("in_" + name, v.shape, F32, kind="ExternalInput").ap() for name, v in arrays.items()]
    out = nc.dram_tensor("out", [B, CH, NWIN * NC * ROW], F32, kind="ExternalOutput").ap()
    preact_block(nc, *aps, out)
    r = _run(nc, [{"in_" + k: v for k, v in arrays.items()}], core_ids=[0])
    return from_windows(r.results[0]["out"])
```
